# Optimizing a Trainium2 kernel written in Bass

```python
import numpy as np
import jax
import jax.numpy as jnp

def _softmax(x, axis=-1):
    return jax.nn.softmax(x, axis=axis)
def _gelu(x):
    return jax.nn.gelu(x, approximate=True)
def _silu(x):
    return jax.nn.silu(x)
def _sigmoid(x):
    return jax.nn.sigmoid(x)
def _layernorm(x, axis=-1, eps=1e-5):
    m = jnp.mean(x, axis=axis, keepdims=True)
    v = jnp.var(x, axis=axis, keepdims=True)
    return (x - m) / jnp.sqrt(v + eps)
def _scatter_add(tgt, idx, src, axis=0):
    return tgt.at[idx].add(src)
def _segment_sum(src, seg, n):
    return jax.ops.segment_sum(src, seg, n)

kernel_name = 'mk_conv_preact_d1_conv_nchw256_8faacb'

def setup_inputs(seed: int = 0):
    np.random.seed(seed)
    _w = jnp.asarray
    def _rec_inputs():
        import jax
        import jax.numpy as jnp
        _gk = jax.random.key(seed)
        x = -0.0003929 + 0.9999 * jax.random.normal(jax.random.fold_in(_gk, 1), (16, 256, 64, 64), jnp.float32)
        return x
    x = _rec_inputs()
    def _L0_conv_setup():
        import jax, jax.numpy as jnp
        import numpy as np
        EPS = 1e-05
        BN_EPS = 1e-05
        key = jax.random.key(seed)
        ks = jax.random.split(key, 7)
        B, C, H, W = (16, 256, 64, 64)
        return {'x': jax.random.normal(ks[0], (B, C, H, W), dtype=jnp.float32), 'w_qkv': jax.random.normal(ks[1], (3 * C, C), dtype=jnp.float32) * C ** (-0.5), 'w_proj': jax.random.normal(ks[2], (C, C), dtype=jnp.float32) * C ** (-0.5), 'bn_gamma': jax.random.uniform(ks[3], (C,), dtype=jnp.float32, minval=0.5, maxval=1.5), 'bn_beta': jax.random.normal(ks[4], (C,), dtype=jnp.float32) * 0.1, 'bn_mean': jax.random.normal(ks[5], (C,), dtype=jnp.float32) * 0.1, 'bn_var': jax.random.uniform(ks[6], (C,), dtype=jnp.float32, minval=0.5, maxval=1.5)}
    _L0_conv_all = _L0_conv_setup()
    _L0_conv_in = {k: v for k, v in _L0_conv_all.items() if k in ('w_qkv', 'w_proj', 'bn_gamma', 'bn_beta', 'bn_mean', 'bn_var', )}
    del _L0_conv_all

    return {
        "x": x,
        "L0_conv_w_qkv": _L0_conv_in["w_qkv"],
        "L0_conv_w_proj": _L0_conv_in["w_proj"],
        "L0_conv_bn_gamma": _L0_conv_in["bn_gamma"],
        "L0_conv_bn_beta": _L0_conv_in["bn_beta"],
        "L0_conv_bn_mean": _L0_conv_in["bn_mean"],
        "L0_conv_bn_var": _L0_conv_in["bn_var"],
    }

def reference(x, L0_conv_w_qkv, L0_conv_w_proj, L0_conv_bn_gamma, L0_conv_bn_beta, L0_conv_bn_mean, L0_conv_bn_var):
    import jax
    import jax.numpy as jnp
    def _L0_conv_ref(x, w_qkv, w_proj, bn_gamma, bn_beta, bn_mean, bn_var):
        import jax, jax.numpy as jnp
        import numpy as np
        EPS = 1e-05
        BN_EPS = 1e-05
        B, C, H, W = x.shape
        N = H * W
        xf = x.reshape(B, C, N)
        qkv = jnp.einsum('oc,bcn->bon', w_qkv, xf)
        qkv = qkv.reshape(B, C, 3, N).transpose(0, 3, 1, 2)
        q = jax.nn.relu(qkv[..., 0])
        k = jax.nn.relu(qkv[..., 1])
        v = qkv[..., 2]
        v = jnp.concatenate([v, jnp.ones((B, N, 1), dtype=v.dtype)], axis=-1)
        kv = jnp.einsum('bnc,bnv->bcv', k, v)
        out = jnp.einsum('bnc,bcv->bnv', q, kv)
        out = out[..., :-1] / (out[..., -1:] + EPS)
        out = out.transpose(0, 2, 1)
        y = jnp.einsum('oc,bcn->bon', w_proj, out)
        scale = bn_gamma / jnp.sqrt(bn_var + BN_EPS)
        y = (y - bn_mean[:, None]) * scale[:, None] + bn_beta[:, None]
        return y.reshape(B, C, H, W)

    def _gn(v, G=32, eps=1e-5):
        B_, C_, H_, W_ = v.shape
        g = v.reshape(B_, G, C_ // G, H_, W_)
        m = jnp.mean(g, axis=(2, 3, 4), keepdims=True)
        s = jnp.var(g, axis=(2, 3, 4), keepdims=True)
        return ((g - m) / jnp.sqrt(s + eps)).reshape(v.shape)

    def _ln_c(v, eps=1e-6):
        m = jnp.mean(v, axis=1, keepdims=True)
        s = jnp.var(v, axis=1, keepdims=True)
        return (v - m) / jnp.sqrt(s + eps)

    def _ln_t(v, eps=1e-5):
        m = jnp.mean(v, axis=-1, keepdims=True)
        s = jnp.var(v, axis=-1, keepdims=True)
        return (v - m) / jnp.sqrt(s + eps)

    def _to_tokens(v):
        B_, C_, H_, W_ = v.shape
        return v.reshape(B_, C_, H_ * W_).transpose(0, 2, 1)
    def _from_tokens(t, like):
        B_, C_, H_, W_ = like.shape
        return t.transpose(0, 2, 1).reshape(B_, C_, H_, W_)

    x = x + _L0_conv_ref(_gn(x), L0_conv_w_qkv, L0_conv_w_proj, L0_conv_bn_gamma, L0_conv_bn_beta, L0_conv_bn_mean, L0_conv_bn_var)
    return x


_drawn_inputs = setup_inputs


def setup_inputs(seed=0):
    import zlib

    import numpy as np

    out = dict(_drawn_inputs(seed))
    spreads = {}
    factors = {'L0_conv_w_qkv': 3.001, 'L0_conv_w_proj': 3.057, 'L0_conv_bn_var': 3.514}
    for name, (base, spread) in spreads.items():
        noise = np.random.default_rng([zlib.crc32(name.encode()), seed]).standard_normal(out[name].shape)
        drawn = base * np.exp(spread * noise) if base else spread * noise
        out[name] = jnp.asarray(drawn.astype(out[name].dtype))
    for name, factor in factors.items():
        out[name] = (out[name] * factor).astype(out[name].dtype)
    return out
```

```python
import concourse.bass as bass
import numpy as np
from concourse import mybir
from contextlib import ExitStack

F32 = mybir.dt.float32
F16 = mybir.dt.float16
ALU = mybir.AluOpType
ACT = mybir.ActivationFunctionType
AX = mybir.AxisListType.X

P = 128
GROUPS = 32
GN_EPS = 1e-5
BN_EPS = 1e-5
ATT_EPS = 1e-5
TINY = 1e-30


def attention_program(nc, x, w_qkv, w_proj, gamma, beta, bn_mean, bn_var, out):
    B, C, HH, WW = x.shape
    N = HH * WW
    H = C // P
    PER = C // GROUPS
    CH = 512
    NCH = N // CH
    PAIR = 2 * P
    NP = N // PAIR
    KAPPA = 1.0 / (4 * N)
    C1 = C + 1
    LO = C + 2

    xd = x.rearrange("b (h p) y z -> b p h (y z)", p=P)
    od = out.rearrange("b (h p) y z -> b p h (y z)", p=P)
    wqkv_d = w_qkv.rearrange("(h p j) i -> p h (j i)", p=P, j=3)
    wproj_d = w_proj.rearrange("(h p) i -> p h i", p=P)

    ctx = ExitStack()
    with ctx:
        def sb(name, shape, dt=F32):
            return ctx.enter_context(nc.sbuf_tensor(name, shape, dt))

        def sem(name):
            return ctx.enter_context(nc.semaphore(name))

        xs = sb("xs", [P, 2, H, N])
        xhi = sb("xhi", [P, 2, H, N], F16)
        xlo = sb("xlo", [P, 2, H, N], F16)
        xn = sb("xn", [P, 2, H, CH])
        khi = sb("khi", [P, 2, 2, C], F16)
        klo = sb("klo", [P, 2, 2, C], F16)
        xt = sb("xt", [P, 2, 2, 2 * LO], F16)
        qhi = sb("qhi", [P, 2, H, CH], F16)
        qlo = sb("qlo", [P, 2, H, CH], F16)
        yt = sb("yt", [P, 2, 2, C])
        rden = sb("rden", [P, 2, 2])
        den = sb("den", [P, 2, 2])
        kx = sb("kx", [P, H, C1])
        kxt = sb("kxt", [P, H, C])
        mt = sb("mt", [P, H, 2, LO], F16)
        w3 = sb("w3", [P, H, 3 * C])
        wp = sb("wp", [P, H, C])
        wn = sb("wn", [P, 2, H, C])
        wqh = sb("wqh", [P, H, C], F16)
        wql = sb("wql", [P, H, C], F16)
        wkh = sb("wkh", [P, H, C], F16)
        wkl = sb("wkl", [P, H, C], F16)
        wpt = sb("wpt", [P, H, C])
        pv = sb("pv", [P, H, C])
        pvt = sb("pvt", [P, H, C])
        ident = sb("ident", [P, P])
        ident16 = sb("ident16", [P, P], F16)
        bn = sb("bn", [P, 4, H])
        rmax = sb("rmax", [P, 2, H])
        rinv = sb("rinv", [P, 2, H])
        pmax = sb("pmax", [P, H])
        pinv = sb("pinv", [P, H])
        rr = sb("rr", [P, H])
        rrm = sb("rrm", [P, 1])
        rall = sb("rall", [P, 1])
        rallc = sb("rallc", [P, 1])
        rallinv = sb("rallinv", [P, 1])
        rho = sb("rho", [P, H])
        deps = sb("deps", [P, 1])
        bs = sb("bs", [P, 8, H])
        oscale = sb("oscale", [P, H])
        obias = sb("obias", [P, H])
        bst = sb("bst", [P, H, NCH, 6])
        cst = sb("cst", [P, 32])
        cstT = sb("cstT", [P, 32])
        gsum = sb("gsum", [P, 32 // PER])
        gexp = sb("gexp", [P, 2, 32])
        gdev = sb("gdev", [P, 32])
        gsq = sb("gsq", [P, 32])
        gsum2 = sb("gsum2", [P, 32 // PER])
        gback = sb("gback", [P, 2, 32])
        gvar = sb("gvar", [P, H])
        gstd = sb("gstd", [P, H])
        nr = sb("nr", [P, 4, H])
        gmean = sb("gmean", [P, H])
        grstd = sb("grstd", [P, H])

        ps = ctx.enter_context(nc.psum_tensor("ps", [P, 8, 512], F32))

        def ps_k(slot):
            return ps[:, 4 + 2 * slot, :].rearrange("p (n c) -> p n c", n=2)

        def ps_xt(slot):
            return ps[:, 5 + 2 * slot, :].bitcast(F16).rearrange("p (n s c) -> p n s c", n=2, s=2)

        ps_kxt = ps[:, 4, :].rearrange("p (g c) -> p g c", g=H)
        ps_m = ps[:, 6, :].rearrange("p (h c) -> p h c", h=H)

        s_w = sem("s_w")
        s_id = sem("s_id")
        s_wabs = sem("s_wabs")
        s_wt = sem("s_wt")
        s_wthi = sem("s_wthi")
        s_wtlo = sem("s_wtlo")
        s_pv = sem("s_pv")
        s_pvn = sem("s_pvn")
        s_rrm = sem("s_rrm")
        s_rall = sem("s_rall")
        s_bnv = sem("s_bnv")
        s_bnsqrt = sem("s_bnsqrt")
        s_consts = sem("s_consts")
        s_set = sem("s_set")
        s_first = [sem(f"s_first{j}") for j in range(NCH)]
        s_load = sem("s_load")
        s_store = sem("s_store")
        s_bst = sem("s_bst")
        s_stat = sem("s_stat")
        s_gvar = sem("s_gvar")
        s_gstd = sem("s_gstd")
        s_xn = sem("s_xn")
        s_xhi = sem("s_xhi")
        s_xlo = sem("s_xlo")
        s_kx = sem("s_kx")
        s_khi = sem("s_khi")
        s_klo = sem("s_klo")
        s_sum = sem("s_sum")
        s_kx0 = sem("s_kx0")
        s_kx1 = sem("s_kx1")
        s_kxT = sem("s_kxT")
        s_kxt = sem("s_kxt")
        s_m = sem("s_m")
        s_mhi = sem("s_mhi")
        s_mlo = sem("s_mlo")
        s_mk = sem("s_mk")
        s_q = sem("s_q")
        s_qhi = sem("s_qhi")
        s_qlo = sem("s_qlo")
        s_y = sem("s_y")
        s_dsum = sem("s_dsum")
        s_rden = sem("s_rden")
        s_yt = sem("s_yt")
        s_fin = sem("s_fin")
        s_out = sem("s_out")
        s_xb = sem("s_xb")

        SET_UP_LOADS = 6
        FIRST_SPLITS = ((2, 3), (4,), (5, 6), (7,))

        block = ctx.enter_context(nc.Block())

        @block.sync
        def _(sp):
            def load(b, slot, c0, landed=s_load):
                sp.dma_start(xs[:, slot, :, bass.ds(c0, CH)],
                             xd[b, :, :, bass.ds(c0, CH)]).then_inc(landed, 16)

            for j in range(NCH):
                load(0, 0, j * CH, s_first[j])
            for j in range(NCH):
                load(1, 1, j * CH)

            def store(b, j, slot):
                sp.wait_ge(s_out, 1 + H * (b * NCH + j + 1))
                sp.dma_start(od[b, :, :, bass.ds(j * CH, CH)],
                             xs[:, slot, :, bass.ds(j * CH, CH)]).then_inc(s_store, 16)

            with sp.Fori(0, B - 2) as b:
                slot = b & 1
                with sp.Fori(0, NCH) as j:
                    sp.wait_ge(s_load, 16 * (NCH * (b + 1) + j))
                    store(b, j, slot)
                    sp.wait_ge(s_store, 16 * (b * NCH + j + 1))
                    load(b + 2, slot, j * CH)
            for b in (B - 2, B - 1):
                with sp.Fori(0, NCH) as j:
                    store(b, j, b & 1)
            sp.wait_ge(s_store, 16 * NCH * B)

        @block.gpsimd
        def _(pool):
            nc.gpsimd.memset(ident[:, :], 0.0).then_inc(s_id, 1)
            pool.wait_ge(s_id, 1)
            nc.gpsimd.affine_select(out=ident[:, :], in_=ident[:, :], compare_op=ALU.not_equal, fill=1.0,
                                    base=0, pattern=[[-1, P]], channel_multiplier=1).then_inc(s_id, 1)
            pool.wait_ge(s_rrm, 1)
            nc.gpsimd.partition_all_reduce(rall[:, :], rrm[:, :], P, bass.bass_isa.ReduceOp.max
                                           ).then_inc(s_rall, 1)

            def split_lo(b, j, slot, buf):
                pool.wait_ge(s_xhi, b * NCH + j + 1)
                nc.gpsimd.tensor_tensor(xlo[:, slot, :, bass.ds(j * CH, CH)], xn[:, buf],
                                        xhi[:, slot, :, bass.ds(j * CH, CH)], ALU.subtract
                                        ).then_inc(s_xlo, 1)

            with pool.Fori(0, B) as b:
                with pool.Fori(0, NCH // 2) as i:
                    split_lo(b, 2 * i, b & 1, 0)
                    split_lo(b, 2 * i + 1, b & 1, 1)

        @block.scalar
        def _(act):
            act.dma_start(w3[:, :, :], wqkv_d).then_inc(s_w, 16)
            act.dma_start(wp[:, :, :], wproj_d).then_inc(s_w, 16)
            for n, v in enumerate((gamma, beta, bn_mean, bn_var)):
                act.dma_start(bn[:, n, :], v.rearrange("(h p) -> p h", p=P),
                              allow_slow_non_contiguous=True).then_inc(s_w, 16)
            for n, dst in enumerate((wqh, wkh, wpt)):
                act.wait_ge(s_wt, n + 1)
                nc.scalar.copy(dst[:, :, :], ps[:, 2 + n, :].rearrange("p (g c) -> p g c", g=H)
                               ).then_inc(s_wthi, 1)
            act.sem_inc(s_yt, 1)
            act.wait_ge(s_bnv, 1)
            nc.scalar.activation(bs[:, 1, :], bs[:, 0, :], ACT.Sqrt).then_inc(s_bnsqrt, 1)
            act.wait_ge(s_wt, 4)
            nc.scalar.copy(pvt[:, :, :], ps[:, 6, :].rearrange("p (g c) -> p g c", g=H)
                           ).then_inc(s_wthi, 1)

            def group_std(b):
                act.wait_ge(s_gvar, b + 1)
                nc.scalar.activation(gstd[:, :], gvar[:, :], ACT.Sqrt).then_inc(s_gstd, 1)

            def split_hi(b, j, slot, buf):
                act.wait_ge(s_xn, b * NCH + j + 1)
                nc.scalar.copy(xhi[:, slot, :, bass.ds(j * CH, CH)], xn[:, buf]).then_inc(s_xhi, 1)

            def k_hi(b, t, slot):
                act.wait_ge(s_kx, b * NP + t + 1)
                if not isinstance(t, int) or t >= 2:
                    act.wait_ge(s_sum, b * NP + t - 1)
                nc.scalar.activation(khi[:, slot], ps_k(slot), ACT.Relu).then_inc(s_khi, 1)

            def add_bias(b, j, slot):
                act.wait_ge(s_xlo, b * NCH + j + 1)
                for h in range(H):
                    last = nc.scalar.activation(xs[:, slot, h, bass.ds(j * CH, CH)],
                                                xs[:, slot, h, bass.ds(j * CH, CH)],
                                                ACT.Identity, bias=obias[:, h:h + 1], scale=1.0)
                last.then_inc(s_xb, 1)

            def q_hi(b, j, h, slot):
                act.wait_ge(s_q, H * (b * NCH + j) + h + 1)
                nc.scalar.activation(qhi[:, slot, h, :], ps[:, 2 + h, :], ACT.Relu).then_inc(s_qhi, 1)

            def divide(b, j, g):
                act.wait_ge(s_rden, 2 * (b * NCH + j) + g + 1)
                for n in range(2):
                    last = nc.scalar.activation(yt[:, g, n, :], ps[:, 4 + 2 * g + n, 0:C], ACT.Copy,
                                                scale=rden[:, g, n:n + 1])
                last.then_inc(s_yt, 1)

            def image(b, prepare, first=False):
                slot, other = b & 1, 1 - (b & 1)
                for t in range(2):
                    k_hi(b, t, t)
                    if first:
                        for j in FIRST_SPLITS[t]:
                            split_hi(0, j, 0, j % 2)
                add_bias(b, 0, slot)
                if first:
                    for t in range(2, 4):
                        k_hi(b, t, t % 2)
                        for j in FIRST_SPLITS[t]:
                            split_hi(0, j, 0, j % 2)
                    add_bias(b, 1, slot)
                with act.Fori(2 if first else 1, NCH - 1) as i:
                    k_hi(b, 2 * i, 0)
                    k_hi(b, 2 * i + 1, 1)
                    add_bias(b, i, slot)
                if prepare:
                    group_std(b + 1)
                k_hi(b, NP - 2, 0)
                k_hi(b, NP - 1, 1)
                add_bias(b, NCH - 1, slot)
                act.wait_ge(s_sum, NP * (b + 1))
                nc.scalar.activation(kx[:, 0, :], ps[:, 0, 0:C1], ACT.Copy,
                                     scale=rho[:, 0:1]).then_inc(s_kx0, 1)
                q_hi(b, 0, 0, 0)
                q_hi(b, 0, 1, 0)
                q_hi(b, 1, 0, 1)
                act.wait_ge(s_m, b + 1)
                nc.scalar.copy(mt[:, :, 0, 0:C], ps_m).then_inc(s_mhi, 1)
                q_hi(b, 1, 1, 1)
                divide(b, 0, 0)
                divide(b, 0, 1)

                def chunk(j, odd, last=False):
                    if not last:
                        q_hi(b, j + 1, 0, 1 - odd)
                    if prepare:
                        split_hi(b + 1, j - 1, other, 1 - odd)
                    divide(b, j, 0)
                    if not last:
                        q_hi(b, j + 1, 1, 1 - odd)
                    divide(b, j, 1)

                with act.Fori(0, NCH // 2 - 1) as i:
                    chunk(2 * i + 1, 1)
                    chunk(2 * i + 2, 0)
                chunk(NCH - 1, 1, last=True)
                if prepare:
                    split_hi(b + 1, NCH - 1, other, 1)

            group_std(0)
            split_hi(0, 0, 0, 0)
            split_hi(0, 1, 0, 1)
            act.wait_ge(s_consts, 1)
            image(0, True, first=True)
            with act.Fori(1, B - 1) as b:
                image(b, True)
            image(B - 1, False)

        @block.vector
        def _(dve):
            set_up = [0]

            def step(ins):
                set_up[0] += 1
                ins.then_inc(s_set, 1)
                dve.wait_ge(s_set, set_up[0])

            V = nc.vector
            V.memset(xt[:, :, :, :], 1.0).then_inc(s_out, 1)
            dve.wait_ge(s_id, 2)
            V.tensor_copy(ident16[:, :], ident[:, :]).then_inc(s_id, 1)
            def weights_scale():
                dve.wait_ge(s_w, 16 * SET_UP_LOADS)
                for h in range(H):
                    step(V.tensor_reduce(rmax[:, :, h], w3[:, h, 0:2 * C].rearrange("p (j i) -> p j i", j=2),
                                         AX, ALU.max, apply_absolute_value=True))
                step(V.tensor_scalar_max(rmax[:, :, :], rmax[:, :, :], TINY))
                step(V.reciprocal(rinv[:, :, :], rmax[:, :, :]))
                for j in range(2):
                    for h in range(H):
                        V.tensor_scalar(wn[:, j, h, :], w3[:, h, j * C:(j + 1) * C], rinv[:, j, h:h + 1], None,
                                        ALU.mult).then_inc(s_wabs, 1)
                step(V.tensor_tensor(rr[:, :], rmax[:, 0, :], rmax[:, 1, :], ALU.mult))
                V.tensor_reduce(rrm[:, :], rr[:, :], AX, ALU.max).then_inc(s_rrm, 1)
                V.tensor_scalar(bs[:, 0, :], bn[:, 3, :], BN_EPS, None, ALU.add).then_inc(s_bnv, 1)

            def split_weights():
                for n, (hi, lo) in enumerate(((wqh, wql), (wkh, wkl))):
                    dve.wait_ge(s_wthi, n + 1)
                    V.tensor_tensor(lo[:, :, :], ps[:, 2 + n, :].rearrange("p (g c) -> p g c", g=H),
                                    hi[:, :, :], ALU.subtract).then_inc(s_wtlo, 1)

            def projection():
                dve.wait_ge(s_pv, 1)
                ps_pv = ps[:, 5, :].rearrange("p (h c) -> p h c", h=H)
                step(V.tensor_reduce(pmax[:, :], ps_pv, AX, ALU.max, apply_absolute_value=True))
                step(V.tensor_scalar_max(pmax[:, :], pmax[:, :], TINY))
                step(V.reciprocal(pinv[:, :], pmax[:, :]))
                for h in range(H):
                    V.tensor_scalar(pv[:, h, :], ps_pv[:, h, :], pinv[:, h:h + 1], None,
                                    ALU.mult).then_inc(s_pvn, 1)

            def vectors():
                dve.wait_ge(s_bnsqrt, 1)
                step(V.reciprocal(bs[:, 2, :], bs[:, 1, :]))
                newton(V, step, bs[:, 2, :], bs[:, 0, :], bs[:, 3, :], bs[:, 4, :], bs[:, 5, :])
                step(V.tensor_tensor(bs[:, 6, :], bs[:, 5, :], bn[:, 0, :], ALU.mult))
                step(V.tensor_tensor(bs[:, 7, :], bs[:, 6, :], bn[:, 2, :], ALU.mult))
                step(V.tensor_tensor(obias[:, :], bn[:, 1, :], bs[:, 7, :], ALU.subtract))
                step(V.tensor_tensor(oscale[:, :], pmax[:, :], bs[:, 6, :], ALU.mult))
                dve.wait_ge(s_rall, 1)
                step(V.tensor_scalar_max(rallc[:, :], rall[:, :], TINY))
                step(V.reciprocal(rallinv[:, :], rallc[:, :]))
                step(V.tensor_scalar(rho[:, :], rr[:, :], rallinv[:, 0:1], KAPPA, ALU.mult, ALU.mult))
                V.tensor_scalar(deps[:, :], rallinv[:, :], ATT_EPS * KAPPA, None, ALU.mult).then_inc(s_consts, 1)
                dve.wait_ge(s_consts, 1)

            def channel_stats(slot, j, h):
                V.bn_stats(bst[:, h, j, :], xs[:, slot, h, bass.ds(j * CH, CH)]).then_inc(s_bst, 1)

            STAT_STEPS = 17

            def group_stats(b):
                done = [0]

                def step(ins, read_next=True):
                    done[0] += 1
                    ins.then_inc(s_stat, 1)
                    if read_next:
                        dve.wait_ge(s_stat, STAT_STEPS * b + done[0])

                def first():
                    dve.wait_ge(s_bst, H * NCH * (b + 1))
                    step(V.memset(cst[:, 2 * H:], 0.0), False)
                    for h in range(H):
                        step(V.bn_aggr(cst[:, 2 * h:2 * h + 2], bst[:, h, :, :].rearrange("p n s -> p (n s)")),
                             h == H - 1)
                    step(V.transpose(cstT[:, :], cst[:, :]))
                    groups = "p (g e) -> p g e"
                    step(V.reduce_sum(gsum[:, :], cstT[:, :].rearrange(groups, e=PER), AX))
                    step(V.tensor_scalar(gexp[:, 0, :].rearrange(groups, e=PER),
                                         gsum[:, :].unsqueeze(2).to_broadcast([P, 32 // PER, PER]),
                                         1.0 / PER, None, ALU.mult))

                def second():
                    groups = "p (g e) -> p g e"
                    step(V.tensor_tensor(gdev[:, :], cstT[:, :], gexp[:, 0, :], ALU.subtract))
                    step(V.tensor_tensor(gsq[:, :], gdev[:, :], gdev[:, :], ALU.mult))
                    step(V.reduce_sum(gsum2[:, :], gsq[:, :].rearrange(groups, e=PER), AX))
                    step(V.tensor_scalar(gexp[:, 1, :].rearrange(groups, e=PER),
                                         gsum2[:, :].unsqueeze(2).to_broadcast([P, 32 // PER, PER]),
                                         1.0 / PER, None, ALU.mult))
                    step(V.transpose(gback[:, :, :].rearrange("p s c -> p (s c)"),
                                     gexp[:, :, :].rearrange("p s c -> p (s c)")))
                    step(V.tensor_copy(gmean[:, :], gback[:, 0, 0:2 * H:2]))
                    V.scalar_tensor_tensor(gvar[:, :], gback[:, 0, 1:2 * H:2], GN_EPS, gback[:, 1, 0:2 * H:2],
                                           ALU.add, ALU.add).then_inc(s_gvar, 1)

                def third():
                    dve.wait_ge(s_gstd, b + 1)
                    step(V.reciprocal(nr[:, 0, :], gstd[:, :]))
                    newton(V, step, nr[:, 0, :], gvar[:, :], nr[:, 1, :], nr[:, 2, :], grstd[:, :])
                    assert done[0] == STAT_STEPS

                return first, second, third

            def normalise(b, j, slot, buf):
                if not isinstance(b, int) or b > 0 or not isinstance(j, int) or j >= 2:
                    dve.wait_ge(s_xlo, b * NCH + j - 1)
                for h in range(H):
                    last = V.tensor_scalar(xn[:, buf, h, :], xs[:, slot, h, bass.ds(j * CH, CH)],
                                           gmean[:, h:h + 1], grstd[:, h:h + 1], ALU.subtract, ALU.mult)
                last.then_inc(s_xn, 1)

            def k_lo(b, t, slot):
                dve.wait_ge(s_kx, b * NP + t + 1)
                if not isinstance(t, int) or t >= 2:
                    dve.wait_ge(s_sum, b * NP + t - 1)
                V.tensor_copy(xt[:, slot].rearrange("p n (s c) -> p n s c", s=2)[:, :, :, 0:C], ps_xt(slot))
                dve.wait_ge(s_khi, b * NP + t + 1)
                V.scalar_tensor_tensor(klo[:, slot], ps_k(slot), 0.0, khi[:, slot],
                                       ALU.max, ALU.subtract).then_inc(s_klo, 1)

            def q_lo(b, j, h, slot):
                dve.wait_ge(s_qhi, H * (b * NCH + j) + h + 1)
                V.scalar_tensor_tensor(qlo[:, slot, h, :], ps[:, 2 + h, :], 0.0, qhi[:, slot, h, :],
                                       ALU.max, ALU.subtract).then_inc(s_qlo, 1)

            def denominators(b, j, g):
                pair = 2 * (b * NCH + j) + g
                dve.wait_ge(s_y, pair + 1)
                V.tensor_scalar(den[:, g, :], ps[:, 4 + 2 * g:6 + 2 * g, C], deps[:, 0:1], None,
                                ALU.add).then_inc(s_dsum, 1)
                dve.wait_ge(s_dsum, pair + 1)
                V.reciprocal(rden[:, g, :], den[:, g, :]).then_inc(s_rden, 1)

            def finish(b, j, slot):
                dve.wait_ge(s_fin, b * NCH + j + 1)
                for h in range(H):
                    V.scalar_tensor_tensor(xs[:, slot, h, bass.ds(j * CH, CH)], ps[:, h, :], oscale[:, h:h + 1],
                                           xs[:, slot, h, bass.ds(j * CH, CH)], ALU.mult, ALU.add
                                           ).then_inc(s_out, 1)

            def image(b, prepare, first=False):
                slot, other = b & 1, 1 - (b & 1)
                for t in range(4):
                    k_lo(b, t, t % 2)
                    if first:
                        for j in FIRST_SPLITS[t]:
                            normalise(0, j, 0, j % 2)
                with dve.Fori(0, NCH // 2) as i:
                    if prepare:
                        dve.wait_ge(s_load, 16 * NCH * (b + 1))
                    for n in range(2):
                        k_lo(b, 2 * i + 4 + n, n)
                        if prepare:
                            for h in range(H):
                                channel_stats(other, 2 * i + n, h)
                stages = group_stats(b + 1) if prepare else ()
                for n in range(4):
                    k_lo(b, NP - 4 + n, n % 2)
                    if prepare and n < 3:
                        stages[n]()
                dve.wait_ge(s_sum, NP * (b + 1))
                V.tensor_scalar(kx[:, 1, :], ps[:, 1, 0:C1], rho[:, 1:2], None, ALU.mult).then_inc(s_kx1, 1)
                dve.wait_ge(s_kx0, b + 1)
                dve.wait_ge(s_kx1, b + 1)
                V.tensor_copy(mt[:, :, 0, C:C1], kx[:, :, C:C1]).then_inc(s_mk, 1)
                dve.wait_ge(s_mk, b + 1)
                V.tensor_tensor(mt[:, :, 1, C:C1], kx[:, :, C:C1], mt[:, :, 0, C:C1], ALU.subtract)
                q_lo(b, 0, 0, 0)
                dve.wait_ge(s_kxT, b + 1)
                V.tensor_copy(kxt[:, :, :], ps_kxt).then_inc(s_kxt, 1)
                q_lo(b, 0, 1, 0)
                q_lo(b, 1, 0, 1)
                dve.wait_ge(s_mhi, b + 1)
                V.tensor_tensor(mt[:, :, 1, 0:C], ps_m, mt[:, :, 0, 0:C], ALU.subtract).then_inc(s_mlo, 1)
                q_lo(b, 1, 1, 1)
                denominators(b, 0, 0)
                denominators(b, 0, 1)
                dve.wait_ge(s_xb, NCH * (b + 1))
                if prepare:
                    normalise(b + 1, 0, other, 0)

                def chunk(j, odd, last=False):
                    if not last:
                        q_lo(b, j + 1, 0, 1 - odd)
                    finish(b, j - 1, slot)
                    denominators(b, j, 0)
                    if prepare:
                        normalise(b + 1, j, other, odd)
                    if not last:
                        q_lo(b, j + 1, 1, 1 - odd)
                    denominators(b, j, 1)

                with dve.Fori(0, NCH // 2 - 1) as i:
                    chunk(2 * i + 1, 1)
                    chunk(2 * i + 2, 0)
                chunk(NCH - 1, 1, last=True)
                finish(b, NCH - 1, slot)

            weights_scale()
            split_weights()
            for j in range(NCH):
                dve.wait_ge(s_first[j], 16)
                for h in range(H):
                    channel_stats(0, j, h)
                if j == NCH // 2:
                    projection()
            for stage in group_stats(0):
                stage()
            for j in range(2):
                normalise(0, j, 0, j % 2)
            vectors()
            image(0, True, first=True)
            with dve.Fori(1, B - 1) as b:
                image(b, True)
            image(B - 1, False)

        @block.tensor
        def _(pe):
            T = nc.tensor

            def turn(bank, src, halves):
                dst = ps[:, bank, :].rearrange("p (g c) -> p g c", g=H)
                for g in range(H):
                    for h in range(halves):
                        last = T.transpose(dst[:, g, h * P:(h + 1) * P], src[:, h, g * P:(g + 1) * P],
                                           ident[:, :])
                return last

            pe.wait_ge(s_id, 3)
            pe.wait_ge(s_wabs, 2)
            turn(2, wn[:, 0], H).then_inc(s_wt, 1)
            pe.wait_ge(s_wabs, 4)
            turn(3, wn[:, 1], H).then_inc(s_wt, 1)
            turn(4, wp, H).then_inc(s_wt, 1)
            pe.wait_ge(s_wthi, 3)
            for h in range(H):
                for g in range(H):
                    last = T.matmul(ps[:, 5, h * C:(h + 1) * C], wpt[:, g, h * P:(h + 1) * P],
                                    w3[:, g, 2 * C:3 * C], start=(g == 0), stop=(g == H - 1))
            last.then_inc(s_pv, 1)
            pe.wait_ge(s_pvn, 2)
            turn(6, pv, H).then_inc(s_wt, 1)
            pe.wait_ge(s_wthi, 4)
            pe.wait_ge(s_wtlo, 2)

            def keys(b, t, slot, odd=None):
                img, n0 = b & 1, t * PAIR
                if slot == 0:
                    pe.wait_ge(s_xlo, b * NCH + (t // 2 if isinstance(t, int) else odd) + 1)
                for n in range(2):
                    at = bass.ds(n0 + n * P, P)
                    k_out, xt_out = ps_k(slot)[:, n, :], ps_xt(slot)[:, n]
                    for g in range(H):
                        hi, lo = xhi[:, img, g, at], xlo[:, img, g, at]
                        T.matmul(k_out, hi, wkh[:, g, :], start=(g == 0), stop=False)
                        T.matmul(k_out, hi, wkl[:, g, :], start=False, stop=False)
                        T.matmul(k_out, lo, wkh[:, g, :], start=False, stop=(g == H - 1))
                    for g in range(H):
                        T.transpose(xt_out[:, 0, g * P:(g + 1) * P], xhi[:, img, g, at], ident16[:, :])
                        last = T.transpose(xt_out[:, 1, g * P:(g + 1) * P], xlo[:, img, g, at], ident16[:, :])
                last.then_inc(s_kx, 1)

            def sums(b, t, slot, first=False, final=False):
                pe.wait_ge(s_klo, b * NP + t + 1)
                for n in range(2):
                    ones = xt[:, slot, n, 0:C1]
                    lo = xt[:, slot, n, LO:LO + C]
                    for h in range(H):
                        kh, kl = khi[:, slot, n, h * P:(h + 1) * P], klo[:, slot, n, h * P:(h + 1) * P]
                        T.matmul(ps[:, h, 0:C1], kh, ones, start=(first and n == 0), stop=False)
                        T.matmul(ps[:, h, 0:C], kh, lo, start=False, stop=False)
                        last = T.matmul(ps[:, h, 0:C1], kl, ones, start=False, stop=(final and n == 1))
                last.then_inc(s_sum, 1)

            def queries(img, j, h):
                at = bass.ds(j * CH, CH)
                for g in range(H):
                    hi, lo = xhi[:, img, g, at], xlo[:, img, g, at]
                    wh, wl = wqh[:, g, h * P:(h + 1) * P], wql[:, g, h * P:(h + 1) * P]
                    T.matmul(ps[:, 2 + h, :], wh, hi, start=(g == 0), stop=False)
                    T.matmul(ps[:, 2 + h, :], wh, lo, start=False, stop=False)
                    last = T.matmul(ps[:, 2 + h, :], wl, hi, start=False, stop=(g == H - 1))
                last.then_inc(s_q, 1)

            def outputs(b, j, g, slot):
                for n in range(2):
                    acc = ps[:, 4 + 2 * g + n, 0:C1]
                    at = slice((2 * g + n) * P, (2 * g + n + 1) * P)
                    for h in range(H):
                        mh, ml = mt[:, h, 0, 0:C1], mt[:, h, 1, 0:C1]
                        T.matmul(acc, qhi[:, slot, h, at], mh, start=(h == 0), stop=False)
                        T.matmul(acc, qhi[:, slot, h, at], ml, start=False, stop=False)
                        last = T.matmul(acc, qlo[:, slot, h, at], mh, start=False, stop=(h == H - 1))
                last.then_inc(s_y, 1)

            def turn_back(b, j):
                pe.wait_ge(s_yt, 1 + 2 * (b * NCH + j + 1))
                for h in range(H):
                    for n in range(4):
                        last = T.transpose(ps[:, h, n * P:(n + 1) * P],
                                           yt[:, n // 2, n % 2, h * P:(h + 1) * P], ident[:, :])
                last.then_inc(s_fin, 1)

            def image(b, last_image=False):
                img = b & 1
                keys(b, 1, 1)
                pe.wait_ge(s_out, 1 + H * NCH * b)
                for t in range(2):
                    sums(b, t, t, first=(t == 0))
                    keys(b, t + 2, t)
                with pe.Fori(1, NCH - 1) as i:
                    for n in range(2):
                        sums(b, 2 * i + n, n)
                        keys(b, 2 * i + n + 2, n, i + 1)
                sums(b, NP - 2, 0)
                sums(b, NP - 1, 1, final=True)

                queries(img, 0, 0)
                queries(img, 0, 1)
                pe.wait_ge(s_kx0, b + 1)
                pe.wait_ge(s_kx1, b + 1)
                turn(4, kx, H).then_inc(s_kxT, 1)
                pe.wait_ge(s_qlo, H * (b * NCH) + 1)
                queries(img, 1, 0)
                pe.wait_ge(s_kxt, b + 1)
                for h in range(H):
                    for g in range(H):
                        last = T.matmul(ps_m[:, h, :], kxt[:, g, h * P:(h + 1) * P], pvt[:, g, :],
                                        start=(g == 0), stop=(g == H - 1))
                last.then_inc(s_m, 1)
                pe.wait_ge(s_qlo, H * (b * NCH) + 2)
                queries(img, 1, 1)
                pe.wait_ge(s_mlo, b + 1)
                pe.wait_ge(s_qlo, H * (b * NCH + 1))
                outputs(b, 0, 0, 0)
                outputs(b, 0, 1, 0)

                def chunk(j, odd, last=False):
                    if not last:
                        pe.wait_ge(s_qlo, H * (b * NCH + j) + 1)
                        queries(img, j + 1, 0)
                    if not isinstance(j, int) or j > 1:
                        pe.wait_ge(s_out, 1 + H * (b * NCH + j - 1))
                    turn_back(b, j - 1)
                    pe.wait_ge(s_qlo, H * (b * NCH + j + 1))
                    outputs(b, j, 0, odd)
                    if not last:
                        queries(img, j + 1, 1)
                    outputs(b, j, 1, odd)

                with pe.Fori(0, NCH // 2 - 1) as i:
                    chunk(2 * i + 1, 1)
                    chunk(2 * i + 2, 0)
                chunk(NCH - 1, 1, last=True)
                if not last_image:
                    pe.wait_ge(s_yt, 2 * NCH * (b + 1))
                    keys(b + 1, 0, 0)
                pe.wait_ge(s_out, 1 + H * (b * NCH + NCH - 1))
                turn_back(b, NCH - 1)

            keys(0, 0, 0)
            with pe.Fori(0, B - 1) as b:
                image(b)
            image(B - 1, last_image=True)


def newton(V, step, r, v, t1, t2, res):
    step(V.tensor_tensor(t1, r, r, ALU.mult))
    step(V.tensor_tensor(t2, t1, v, ALU.mult))
    step(V.tensor_scalar(t1, t2, -0.5, 1.5, ALU.mult, ALU.add))
    step(V.tensor_tensor(res, r, t1, ALU.mult))


_INS = ["x", "L0_conv_w_qkv", "L0_conv_w_proj", "L0_conv_bn_gamma", "L0_conv_bn_beta", "L0_conv_bn_mean",
        "L0_conv_bn_var"]


def kernel(**inputs):
    import concourse.bacc as bacc
    from concourse.bass_utils import run_bass_kernel_spmd

    nc = bacc.Bacc("TRN2", target_bir_lowering=False, num_devices=1)
    arrays, args = {}, []
    for name in _INS:
        a = np.ascontiguousarray(inputs[name])
        arrays[f"in_{name}"] = a
        args.append(nc.dram_tensor(f"in_{name}", a.shape, mybir.dt.from_np(a.dtype), kind="ExternalInput").ap())
    out = nc.dram_tensor("out_0", arrays["in_x"].shape, F32, kind="ExternalOutput").ap()
    attention_program(nc, *args, out)
    r = run_bass_kernel_spmd(nc, [arrays], core_ids=[0])
    return r.results[0]["out_0"]
```

```python
import concourse.bass as bass
import numpy as np
from concourse import mybir
from contextlib import ExitStack

F32 = mybir.dt.float32
F16 = mybir.dt.float16
ALU = mybir.AluOpType
ACT = mybir.ActivationFunctionType
AX = mybir.AxisListType.X

P = 128
GROUPS = 32
GN_EPS = 1e-5
BN_EPS = 1e-5
ATT_EPS = 1e-5
TINY = 1e-30


def attention_program(nc, x, w_qkv, w_proj, gamma, beta, bn_mean, bn_var, out):
    B, C, HH, WW = x.shape
    N = HH * WW
    H = C // P
    PER = C // GROUPS
    CH = 512
    NCH = N // CH
    PAIR = 2 * P
    NP = N // PAIR
    KAPPA = 1.0 / (4 * N)
    C1 = C + 1
    CB = CH // P
    P1 = P + 1
    TP = P + 16

    xd = x.rearrange("b (h p) y z -> b p h (y z)", p=P)
    od = out.rearrange("b (h p) y z -> b p h (y z)", p=P)
    wqkv_d = w_qkv.rearrange("(h p j) i -> p h (j i)", p=P, j=3)
    wproj_d = w_proj.rearrange("(h p) i -> p h i", p=P)

    ctx = ExitStack()
    with ctx:
        def sb(name, shape, dt=F32):
            return ctx.enter_context(nc.sbuf_tensor(name, shape, dt))

        def sem(name):
            return ctx.enter_context(nc.semaphore(name))

        xs = sb("xs", [P, 2, H, N])
        xsp = sb("xsp", [P, 2, NCH, 2, H, CH], F16)
        xn = sb("xn", [P, 2, H, CH])
        khi = sb("khi", [P, 2, 2, C], F16)
        klo = sb("klo", [P, 2, 2, C], F16)
        xt = sb("xt", [P, NCH, 2, H, CB, TP], F16)
        work = sb("work", [P, 16 * C])
        yt = work[:, 0:8 * C].rearrange("p (s g n c) -> p s g n c", s=2, g=2, n=2)
        q_split = work[:, 8 * C:16 * C].bitcast(F16).rearrange("p (l s h c) -> p l s h c", l=2, s=2, h=H)
        qhi, qlo = q_split[:, 0], q_split[:, 1]
        w3 = work[:, 0:6 * C].rearrange("p (h c) -> p h c", h=H)
        wn = work[:, 6 * C:10 * C].rearrange("p (j h c) -> p j h c", j=2, h=H)
        wp = work[:, 10 * C:12 * C].rearrange("p (h c) -> p h c", h=H)
        wpt = work[:, 12 * C:14 * C].rearrange("p (h c) -> p h c", h=H)
        pv = work[:, 14 * C:16 * C].rearrange("p (h c) -> p h c", h=H)
        rden = sb("rden", [P, 2, 2])
        den = sb("den", [P, 2, 2])
        kx = sb("kx", [P, H, H, P1])
        kxt = sb("kxt", [P, H, C])
        mt = sb("mt", [P, H, 2, C + 2], F16)
        wqh = sb("wqh", [P, H, C], F16)
        wql = sb("wql", [P, H, C], F16)
        wkh = sb("wkh", [P, H, C], F16)
        wkl = sb("wkl", [P, H, C], F16)
        pvt = sb("pvt", [P, H, C])
        ident = sb("ident", [P, P])
        bn = sb("bn", [P, 4, H])
        rmax = sb("rmax", [P, 2, H])
        rinv = sb("rinv", [P, 2, H])
        pmax = sb("pmax", [P, H])
        pinv = sb("pinv", [P, H])
        rr = sb("rr", [P, H])
        rrm = sb("rrm", [P, 1])
        rall = sb("rall", [P, 1])
        rallc = sb("rallc", [P, 1])
        rallinv = sb("rallinv", [P, 1])
        rho = sb("rho", [P, H])
        deps = sb("deps", [P, 1])
        bs = sb("bs", [P, 8, H])
        oscale = sb("oscale", [P, H])
        obias = sb("obias", [P, H])
        bst = sb("bst", [P, H, NCH, 6])
        cst = sb("cst", [P, 32])
        cstT = sb("cstT", [P, 32])
        gsum = sb("gsum", [P, 32 // PER])
        gexp = sb("gexp", [P, 2, 32])
        gdev = sb("gdev", [P, 32])
        gsq = sb("gsq", [P, 32])
        gsum2 = sb("gsum2", [P, 32 // PER])
        gback = sb("gback", [P, 2, 32])
        gvar = sb("gvar", [P, H])
        gstd = sb("gstd", [P, H])
        nr = sb("nr", [P, 4, H])
        gmean = sb("gmean", [P, H])
        grstd = sb("grstd", [P, H])

        ps = ctx.enter_context(nc.psum_tensor("ps", [P, 8, 512], F32))

        def ps_k(slot):
            return ps[:, 4 + 2 * slot, :].rearrange("p (n c) -> p n c", n=2)

        def ps_sum(h):
            return ps[:, h, 0:H * P1].rearrange("p (g c) -> p g c", g=H)

        ps_kxt = ps[:, 4, :].rearrange("p (g c) -> p g c", g=H)
        ps_m = ps[:, 6, :].rearrange("p (h c) -> p h c", h=H)

        s_w3 = sem("s_w3")
        s_w = sem("s_w")
        s_id = sem("s_id")
        s_wabs = sem("s_wabs")
        s_wt = sem("s_wt")
        s_wthi = sem("s_wthi")
        s_wtlo = sem("s_wtlo")
        s_pv = sem("s_pv")
        s_pvn = sem("s_pvn")
        s_rrm = sem("s_rrm")
        s_rall = sem("s_rall")
        s_bnv = sem("s_bnv")
        s_bnsqrt = sem("s_bnsqrt")
        s_consts = sem("s_consts")
        s_set = sem("s_set")
        s_first = [sem(f"s_first{j}") for j in range(NCH)]
        s_load = sem("s_load")
        s_store = sem("s_store")
        s_bst = sem("s_bst")
        s_stat = sem("s_stat")
        s_gvar = sem("s_gvar")
        s_gstd = sem("s_gstd")
        s_xn = sem("s_xn")
        s_xhi = sem("s_xhi")
        s_xlo = sem("s_xlo")
        s_stood = sem("s_stood")
        s_xt = sem("s_xt")
        s_kx = sem("s_kx")
        s_khi = sem("s_khi")
        s_klo = sem("s_klo")
        s_sum = sem("s_sum")
        s_kx0 = sem("s_kx0")
        s_kx1 = sem("s_kx1")
        s_kxT = sem("s_kxT")
        s_kxt = sem("s_kxt")
        s_m = sem("s_m")
        s_mhi = sem("s_mhi")
        s_mlo = sem("s_mlo")
        s_mk = sem("s_mk")
        s_q = sem("s_q")
        s_qhi = sem("s_qhi")
        s_qlo = sem("s_qlo")
        s_y = sem("s_y")
        s_dsum = sem("s_dsum")
        s_rden = sem("s_rden")
        s_yt = sem("s_yt")
        s_fin = sem("s_fin")
        s_out = sem("s_out")
        s_xb = sem("s_xb")

        SMALL_LOADS = 5
        FIRST_SPLITS = ((4,), (5,), (6,), (7,))

        block = ctx.enter_context(nc.Block())

        @block.sync
        def _(sp):
            def load(b, slot, c0, landed=s_load):
                sp.dma_start(xs[:, slot, :, bass.ds(c0, CH)],
                             xd[b, :, :, bass.ds(c0, CH)]).then_inc(landed, 16)

            def transpose(b, j, slot):
                sp.wait_ge(s_xlo, NCH * b + j + 1)
                sp.sem_inc(s_stood, 1)
                if not isinstance(b, int) or b:
                    sp.wait_ge(s_sum, NP * b)
                    sp.sem_inc(s_stood, 1)
                if not isinstance(b, int) or b or j:
                    sp.wait_ge(s_xt, 16 * (NCH * b + j))
                    sp.sem_inc(s_stood, 1)
                sp.dma_start_transpose(xt[:, j].rearrange("p s h n c -> p (s h n) c")[:, :, 0:P],
                                       xsp[:, slot, j].rearrange("p s h c -> p (s h c)")
                                       ).then_inc(s_xt, 16)

            def store(b, j, slot):
                sp.wait_ge(s_out, 2 + H * (b * NCH + j + 1))
                sp.dma_start(od[b, :, :, bass.ds(j * CH, CH)],
                             xs[:, slot, :, bass.ds(j * CH, CH)]).then_inc(s_store, 16)

            sp.dma_start(w3[:, :, :], wqkv_d).then_inc(s_w3, 16)
            for j in range(NCH):
                load(0, 0, j * CH, s_first[j])
            for j in range(NCH):
                transpose(0, j, 0)
                if j:
                    sp.wait_ge(s_load, 16 * j)
                load(1, 1, j * CH)

            with sp.Fori(0, B - 2) as b:
                slot = b & 1
                with sp.Fori(0, NCH) as j:
                    transpose(b + 1, j, 1 - slot)
                    store(b, j, slot)
                    sp.wait_ge(s_load, 16 * (NCH * (b + 1) + j))
                    sp.sem_inc(s_stood, 1)
                    sp.wait_ge(s_store, 16 * (b * NCH + j + 1))
                    load(b + 2, slot, j * CH)
            with sp.Fori(0, NCH) as j:
                transpose(B - 1, j, (B - 1) & 1)
                store(B - 2, j, (B - 2) & 1)
            with sp.Fori(0, NCH) as j:
                store(B - 1, j, (B - 1) & 1)
            sp.wait_ge(s_store, 16 * NCH * B)

        @block.gpsimd
        def _(pool):
            nc.gpsimd.memset(ident[:, :], 0.0).then_inc(s_id, 1)
            pool.wait_ge(s_id, 1)
            nc.gpsimd.affine_select(out=ident[:, :], in_=ident[:, :], compare_op=ALU.not_equal, fill=1.0,
                                    base=0, pattern=[[-1, P]], channel_multiplier=1).then_inc(s_id, 1)
            pool.wait_ge(s_rrm, 1)
            nc.gpsimd.partition_all_reduce(rall[:, :], rrm[:, :], P, bass.bass_isa.ReduceOp.max
                                           ).then_inc(s_rall, 1)

            def split_lo(b, j, slot, buf):
                pool.wait_ge(s_xhi, b * NCH + j + 1)
                nc.gpsimd.tensor_tensor(xsp[:, slot, j, 1], xn[:, buf], xsp[:, slot, j, 0], ALU.subtract
                                        ).then_inc(s_xlo, 1)

            with pool.Fori(0, B) as b:
                with pool.Fori(0, NCH // 2) as i:
                    split_lo(b, 2 * i, b & 1, 0)
                    split_lo(b, 2 * i + 1, b & 1, 1)

        @block.scalar
        def _(act):
            act.dma_start(wp[:, :, :], wproj_d).then_inc(s_w, 16)
            for n, v in enumerate((gamma, beta, bn_mean, bn_var)):
                act.dma_start(bn[:, n, :], v.rearrange("(h p) -> p h", p=P),
                              allow_slow_non_contiguous=True).then_inc(s_w, 16)
            for n, dst in enumerate((wqh, wkh, wpt)):
                act.wait_ge(s_wt, n + 1)
                nc.scalar.copy(dst[:, :, :], ps[:, 2 + n, :].rearrange("p (g c) -> p g c", g=H)
                               ).then_inc(s_wthi, 1)
            act.sem_inc(s_yt, 1)
            act.wait_ge(s_bnv, 1)
            nc.scalar.activation(bs[:, 1, :], bs[:, 0, :], ACT.Sqrt).then_inc(s_bnsqrt, 1)
            act.wait_ge(s_wt, 4)
            nc.scalar.copy(pvt[:, :, :], ps[:, 6, :].rearrange("p (g c) -> p g c", g=H)
                           ).then_inc(s_wthi, 1)

            def group_std(b):
                act.wait_ge(s_gvar, b + 1)
                nc.scalar.activation(gstd[:, :], gvar[:, :], ACT.Sqrt).then_inc(s_gstd, 1)

            def split_hi(b, j, slot, buf):
                act.wait_ge(s_xn, b * NCH + j + 1)
                nc.scalar.copy(xsp[:, slot, j, 0], xn[:, buf]).then_inc(s_xhi, 1)

            def k_hi(b, t, slot):
                act.wait_ge(s_kx, b * NP + t + 1)
                if not isinstance(t, int) or t >= 2:
                    act.wait_ge(s_sum, b * NP + t - 1)
                nc.scalar.activation(khi[:, slot], ps_k(slot), ACT.Relu).then_inc(s_khi, 1)

            def add_bias(b, j, slot):
                act.wait_ge(s_xlo, b * NCH + j + 1)
                for h in range(H):
                    last = nc.scalar.activation(xs[:, slot, h, bass.ds(j * CH, CH)],
                                                xs[:, slot, h, bass.ds(j * CH, CH)],
                                                ACT.Identity, bias=obias[:, h:h + 1], scale=1.0)
                last.then_inc(s_xb, 1)

            def q_hi(b, j, h, slot):
                act.wait_ge(s_q, H * (b * NCH + j) + h + 1)
                nc.scalar.activation(qhi[:, slot, h, :], ps[:, 2 + h, :], ACT.Relu).then_inc(s_qhi, 1)

            def divide(b, j, g, slot):
                act.wait_ge(s_rden, 2 * (b * NCH + j) + g + 1)
                for n in range(2):
                    last = nc.scalar.activation(yt[:, slot, g, n, :], ps[:, 4 + 2 * g + n, 0:C], ACT.Copy,
                                                scale=rden[:, g, n:n + 1])
                last.then_inc(s_yt, 1)

            def image(b, prepare, first=False):
                slot, other = b & 1, 1 - (b & 1)
                for t in range(2):
                    k_hi(b, t, t)
                    if first:
                        for j in FIRST_SPLITS[t]:
                            split_hi(0, j, 0, j % 2)
                add_bias(b, 0, slot)
                if first:
                    for t in range(2, 4):
                        k_hi(b, t, t % 2)
                        for j in FIRST_SPLITS[t]:
                            split_hi(0, j, 0, j % 2)
                    add_bias(b, 1, slot)
                with act.Fori(2 if first else 1, NCH - 1) as i:
                    k_hi(b, 2 * i, 0)
                    k_hi(b, 2 * i + 1, 1)
                    add_bias(b, i, slot)
                if prepare:
                    group_std(b + 1)
                k_hi(b, NP - 2, 0)
                k_hi(b, NP - 1, 1)
                add_bias(b, NCH - 1, slot)
                act.wait_ge(s_sum, NP * (b + 1))
                nc.scalar.activation(kx[:, 0], ps_sum(0), ACT.Copy,
                                     scale=rho[:, 0:1]).then_inc(s_kx0, 1)
                q_hi(b, 0, 0, 0)
                q_hi(b, 0, 1, 0)
                q_hi(b, 1, 0, 1)
                act.wait_ge(s_m, b + 1)
                nc.scalar.copy(mt[:, :, 0, 0:C], ps_m).then_inc(s_mhi, 1)
                q_hi(b, 1, 1, 1)
                divide(b, 0, 0, 0)
                divide(b, 0, 1, 0)

                def chunk(j, odd, last=False):
                    if not last:
                        q_hi(b, j + 1, 0, 1 - odd)
                    if prepare:
                        split_hi(b + 1, j - 1, other, 1 - odd)
                    divide(b, j, 0, odd)
                    if not last:
                        q_hi(b, j + 1, 1, 1 - odd)
                    divide(b, j, 1, odd)

                with act.Fori(0, NCH // 2 - 1) as i:
                    chunk(2 * i + 1, 1)
                    chunk(2 * i + 2, 0)
                chunk(NCH - 1, 1, last=True)
                if prepare:
                    split_hi(b + 1, NCH - 1, other, 1)

            group_std(0)
            for j in range(4):
                split_hi(0, j, 0, j % 2)
            act.wait_ge(s_consts, 1)
            image(0, True, first=True)
            with act.Fori(1, B - 1) as b:
                image(b, True)
            image(B - 1, False)

        @block.vector
        def _(dve):
            set_up = [0]

            def step(ins):
                set_up[0] += 1
                ins.then_inc(s_set, 1)
                dve.wait_ge(s_set, set_up[0])

            V = nc.vector
            for n in range(2):
                V.memset(xt[:, n * NCH // 2:(n + 1) * NCH // 2].rearrange("p j s h n c -> p (j s h n) c")[:, :, P:P1],
                         1.0).then_inc(s_out, 1)

            def weights_scale():
                dve.wait_ge(s_w3, 16)
                for h in range(H):
                    step(V.tensor_reduce(rmax[:, :, h], w3[:, h, 0:2 * C].rearrange("p (j i) -> p j i", j=2),
                                         AX, ALU.max, apply_absolute_value=True))
                step(V.tensor_scalar_max(rmax[:, :, :], rmax[:, :, :], TINY))
                step(V.reciprocal(rinv[:, :, :], rmax[:, :, :]))
                for j in range(2):
                    for h in range(H):
                        V.tensor_scalar(wn[:, j, h, :], w3[:, h, j * C:(j + 1) * C], rinv[:, j, h:h + 1], None,
                                        ALU.mult).then_inc(s_wabs, 1)
                step(V.tensor_tensor(rr[:, :], rmax[:, 0, :], rmax[:, 1, :], ALU.mult))
                V.tensor_reduce(rrm[:, :], rr[:, :], AX, ALU.max).then_inc(s_rrm, 1)
                dve.wait_ge(s_w, 16 * SMALL_LOADS)
                V.tensor_scalar(bs[:, 0, :], bn[:, 3, :], BN_EPS, None, ALU.add).then_inc(s_bnv, 1)

            def split_weights():
                for n, (hi, lo) in enumerate(((wqh, wql), (wkh, wkl))):
                    dve.wait_ge(s_wthi, n + 1)
                    V.tensor_tensor(lo[:, :, :], ps[:, 2 + n, :].rearrange("p (g c) -> p g c", g=H),
                                    hi[:, :, :], ALU.subtract).then_inc(s_wtlo, 1)

            def projection():
                dve.wait_ge(s_pv, 1)
                ps_pv = ps[:, 5, :].rearrange("p (h c) -> p h c", h=H)
                step(V.tensor_reduce(pmax[:, :], ps_pv, AX, ALU.max, apply_absolute_value=True))
                step(V.tensor_scalar_max(pmax[:, :], pmax[:, :], TINY))
                step(V.reciprocal(pinv[:, :], pmax[:, :]))
                for h in range(H):
                    V.tensor_scalar(pv[:, h, :], ps_pv[:, h, :], pinv[:, h:h + 1], None,
                                    ALU.mult).then_inc(s_pvn, 1)

            def vectors():
                dve.wait_ge(s_bnsqrt, 1)
                step(V.reciprocal(bs[:, 2, :], bs[:, 1, :]))
                newton(V, step, bs[:, 2, :], bs[:, 0, :], bs[:, 3, :], bs[:, 4, :], bs[:, 5, :])
                step(V.tensor_tensor(bs[:, 6, :], bs[:, 5, :], bn[:, 0, :], ALU.mult))
                step(V.tensor_tensor(bs[:, 7, :], bs[:, 6, :], bn[:, 2, :], ALU.mult))
                step(V.tensor_tensor(obias[:, :], bn[:, 1, :], bs[:, 7, :], ALU.subtract))
                step(V.tensor_tensor(oscale[:, :], pmax[:, :], bs[:, 6, :], ALU.mult))
                dve.wait_ge(s_rall, 1)
                step(V.tensor_scalar_max(rallc[:, :], rall[:, :], TINY))
                step(V.reciprocal(rallinv[:, :], rallc[:, :]))
                step(V.tensor_scalar(rho[:, :], rr[:, :], rallinv[:, 0:1], KAPPA, ALU.mult, ALU.mult))
                V.tensor_scalar(deps[:, :], rallinv[:, :], ATT_EPS * KAPPA, None, ALU.mult).then_inc(s_consts, 1)
                dve.wait_ge(s_consts, 1)

            def channel_stats(slot, j, h):
                V.bn_stats(bst[:, h, j, :], xs[:, slot, h, bass.ds(j * CH, CH)]).then_inc(s_bst, 1)

            STAT_STEPS = 17

            def group_stats(b):
                done = [0]

                def step(ins, read_next=True):
                    done[0] += 1
                    ins.then_inc(s_stat, 1)
                    if read_next:
                        dve.wait_ge(s_stat, STAT_STEPS * b + done[0])

                def first():
                    dve.wait_ge(s_bst, H * NCH * (b + 1))
                    step(V.memset(cst[:, 2 * H:], 0.0), False)
                    for h in range(H):
                        step(V.bn_aggr(cst[:, 2 * h:2 * h + 2], bst[:, h, :, :].rearrange("p n s -> p (n s)")),
                             h == H - 1)
                    step(V.transpose(cstT[:, :], cst[:, :]))
                    groups = "p (g e) -> p g e"
                    step(V.reduce_sum(gsum[:, :], cstT[:, :].rearrange(groups, e=PER), AX))
                    step(V.tensor_scalar(gexp[:, 0, :].rearrange(groups, e=PER),
                                         gsum[:, :].unsqueeze(2).to_broadcast([P, 32 // PER, PER]),
                                         1.0 / PER, None, ALU.mult))

                def second():
                    groups = "p (g e) -> p g e"
                    step(V.tensor_tensor(gdev[:, :], cstT[:, :], gexp[:, 0, :], ALU.subtract))
                    step(V.tensor_tensor(gsq[:, :], gdev[:, :], gdev[:, :], ALU.mult))
                    step(V.reduce_sum(gsum2[:, :], gsq[:, :].rearrange(groups, e=PER), AX))
                    step(V.tensor_scalar(gexp[:, 1, :].rearrange(groups, e=PER),
                                         gsum2[:, :].unsqueeze(2).to_broadcast([P, 32 // PER, PER]),
                                         1.0 / PER, None, ALU.mult))
                    step(V.transpose(gback[:, :, :].rearrange("p s c -> p (s c)"),
                                     gexp[:, :, :].rearrange("p s c -> p (s c)")))
                    step(V.tensor_copy(gmean[:, :], gback[:, 0, 0:2 * H:2]))
                    V.scalar_tensor_tensor(gvar[:, :], gback[:, 0, 1:2 * H:2], GN_EPS, gback[:, 1, 0:2 * H:2],
                                           ALU.add, ALU.add).then_inc(s_gvar, 1)

                def third():
                    dve.wait_ge(s_gstd, b + 1)
                    step(V.reciprocal(nr[:, 0, :], gstd[:, :]))
                    newton(V, step, nr[:, 0, :], gvar[:, :], nr[:, 1, :], nr[:, 2, :], grstd[:, :])
                    assert done[0] == STAT_STEPS

                return first, second, third

            def normalise(b, j, slot, buf):
                if not isinstance(b, int) or b > 0 or not isinstance(j, int) or j >= 2:
                    dve.wait_ge(s_xlo, b * NCH + j - 1)
                for h in range(H):
                    last = V.tensor_scalar(xn[:, buf, h, :], xs[:, slot, h, bass.ds(j * CH, CH)],
                                           gmean[:, h:h + 1], grstd[:, h:h + 1], ALU.subtract, ALU.mult)
                last.then_inc(s_xn, 1)

            def k_lo(b, t, slot):
                dve.wait_ge(s_khi, b * NP + t + 1)
                V.scalar_tensor_tensor(klo[:, slot], ps_k(slot), 0.0, khi[:, slot],
                                       ALU.max, ALU.subtract).then_inc(s_klo, 1)

            def q_lo(b, j, h, slot):
                dve.wait_ge(s_qhi, H * (b * NCH + j) + h + 1)
                V.scalar_tensor_tensor(qlo[:, slot, h, :], ps[:, 2 + h, :], 0.0, qhi[:, slot, h, :],
                                       ALU.max, ALU.subtract).then_inc(s_qlo, 1)

            def denominators(b, j, g):
                pair = 2 * (b * NCH + j) + g
                dve.wait_ge(s_y, pair + 1)
                V.tensor_scalar(den[:, g, :], ps[:, 4 + 2 * g:6 + 2 * g, C], deps[:, 0:1], None,
                                ALU.add).then_inc(s_dsum, 1)
                dve.wait_ge(s_dsum, pair + 1)
                V.reciprocal(rden[:, g, :], den[:, g, :]).then_inc(s_rden, 1)

            def finish(b, j, slot):
                dve.wait_ge(s_fin, b * NCH + j + 1)
                for h in range(H):
                    V.scalar_tensor_tensor(xs[:, slot, h, bass.ds(j * CH, CH)], ps[:, h, :], oscale[:, h:h + 1],
                                           xs[:, slot, h, bass.ds(j * CH, CH)], ALU.mult, ALU.add
                                           ).then_inc(s_out, 1)

            def image(b, prepare, first=False):
                slot, other = b & 1, 1 - (b & 1)
                for t in range(4):
                    if t:
                        k_lo(b, t, t % 2)
                    if first:
                        for j in FIRST_SPLITS[t]:
                            normalise(0, j, 0, j % 2)
                with dve.Fori(0, NCH // 2) as i:
                    for n in range(2):
                        k_lo(b, 2 * i + 4 + n, n)
                        if prepare:
                            dve.wait_ge(s_load, 16 * (NCH * b + 2 * i + n + 1))
                            for h in range(H):
                                channel_stats(other, 2 * i + n, h)
                stages = group_stats(b + 1) if prepare else ()
                for n in range(4):
                    k_lo(b, NP - 4 + n, n % 2)
                    if prepare and n < 3:
                        stages[n]()
                dve.wait_ge(s_sum, NP * (b + 1))
                V.tensor_scalar(kx[:, 1], ps_sum(1), rho[:, 1:2], None, ALU.mult).then_inc(s_kx1, 1)
                dve.wait_ge(s_kx0, b + 1)
                dve.wait_ge(s_kx1, b + 1)
                V.tensor_copy(mt[:, :, 0, C:C1], kx[:, :, 0, P:P1]).then_inc(s_mk, 1)
                dve.wait_ge(s_mk, b + 1)
                V.tensor_tensor(mt[:, :, 1, C:C1], kx[:, :, 0, P:P1], mt[:, :, 0, C:C1], ALU.subtract)
                q_lo(b, 0, 0, 0)
                dve.wait_ge(s_kxT, b + 1)
                V.tensor_copy(kxt[:, :, :], ps_kxt).then_inc(s_kxt, 1)
                q_lo(b, 0, 1, 0)
                q_lo(b, 1, 0, 1)
                dve.wait_ge(s_mhi, b + 1)
                V.tensor_tensor(mt[:, :, 1, 0:C], ps_m, mt[:, :, 0, 0:C], ALU.subtract).then_inc(s_mlo, 1)
                q_lo(b, 1, 1, 1)
                denominators(b, 0, 0)
                denominators(b, 0, 1)
                dve.wait_ge(s_xb, NCH * (b + 1))
                if prepare:
                    normalise(b + 1, 0, other, 0)

                def chunk(j, odd, last=False):
                    if not last:
                        q_lo(b, j + 1, 0, 1 - odd)
                    denominators(b, j, 0)
                    if prepare:
                        normalise(b + 1, j, other, odd)
                    finish(b, j - 1, slot)
                    if not last:
                        q_lo(b, j + 1, 1, 1 - odd)
                    denominators(b, j, 1)

                with dve.Fori(0, NCH // 2 - 1) as i:
                    chunk(2 * i + 1, 1)
                    chunk(2 * i + 2, 0)
                chunk(NCH - 1, 1, last=True)
                if prepare:
                    k_lo(b + 1, 0, 0)
                finish(b, NCH - 1, slot)

            weights_scale()
            split_weights()
            for j in range(NCH):
                dve.wait_ge(s_first[j], 16)
                for h in range(H):
                    channel_stats(0, j, h)
                if j == NCH // 2:
                    projection()
            for stage in group_stats(0):
                stage()
            for j in range(2):
                normalise(0, j, 0, j % 2)
            vectors()
            for j in range(2, 4):
                normalise(0, j, 0, j % 2)
            k_lo(0, 0, 0)
            image(0, True, first=True)
            with dve.Fori(1, B - 1) as b:
                image(b, True)
            image(B - 1, False)

        @block.tensor
        def _(pe):
            T = nc.tensor

            def halves(src):
                return src.rearrange("p h (g c) -> p h g c", g=H)

            def turn(bank, src):
                dst = ps[:, bank, :].rearrange("p (g c) -> p g c", g=H)
                for g in range(H):
                    for h in range(H):
                        last = T.transpose(dst[:, g, h * P:(h + 1) * P], src[:, h, g, :], ident[:, :])
                return last

            pe.wait_ge(s_id, 2)
            pe.wait_ge(s_wabs, 2)
            turn(2, halves(wn[:, 0])).then_inc(s_wt, 1)
            pe.wait_ge(s_wabs, 4)
            turn(3, halves(wn[:, 1])).then_inc(s_wt, 1)
            pe.wait_ge(s_w, 16 * SMALL_LOADS)
            turn(4, halves(wp)).then_inc(s_wt, 1)
            pe.wait_ge(s_wthi, 3)
            for h in range(H):
                for g in range(H):
                    last = T.matmul(ps[:, 5, h * C:(h + 1) * C], wpt[:, g, h * P:(h + 1) * P],
                                    w3[:, g, 2 * C:3 * C], start=(g == 0), stop=(g == H - 1))
            last.then_inc(s_pv, 1)
            pe.wait_ge(s_pvn, 2)
            turn(6, halves(pv)).then_inc(s_wt, 1)
            pe.wait_ge(s_wthi, 4)
            pe.wait_ge(s_wtlo, 2)

            def keys(b, j, slot):
                if slot == 0:
                    pe.wait_ge(s_xlo, b * NCH + j + 1)
                x_hi, x_lo = xsp[:, b & 1, j, 0], xsp[:, b & 1, j, 1]
                for n in range(2):
                    at = slice((2 * slot + n) * P, (2 * slot + n + 1) * P)
                    k_out = ps_k(slot)[:, n, :]
                    for g in range(H):
                        T.matmul(k_out, x_hi[:, g, at], wkh[:, g, :], start=(g == 0), stop=False)
                        T.matmul(k_out, x_hi[:, g, at], wkl[:, g, :], start=False, stop=False)
                        last = T.matmul(k_out, x_lo[:, g, at], wkh[:, g, :], start=False, stop=(g == H - 1))
                last.then_inc(s_kx, 1)

            def sums(b, j, slot, first=False, final=False):
                if first:
                    pe.wait_ge(s_out, 1 + H * NCH * b)
                if slot == 0:
                    pe.wait_ge(s_xt, 16 * (b * NCH + j + 1))
                pe.wait_ge(s_klo, b * NP + 2 * j + slot + 1)
                for n in range(2):
                    ones = xt[:, j, 0, :, 2 * slot + n, 0:P1]
                    lo = xt[:, j, 1, :, 2 * slot + n, 0:P]
                    for h in range(H):
                        if first and n == 0 and h == 1:
                            pe.wait_ge(s_out, 2 + H * NCH * b)
                        kh, kl = khi[:, slot, n, h * P:(h + 1) * P], klo[:, slot, n, h * P:(h + 1) * P]
                        T.matmul(ps_sum(h), kh, ones, start=(first and n == 0), stop=False)
                        T.matmul(ps_sum(h)[:, :, 0:P], kh, lo, start=False, stop=False)
                        last = T.matmul(ps_sum(h), kl, ones, start=False, stop=(final and n == 1))
                last.then_inc(s_sum, 1)

            def queries(img, j, h):
                for g in range(H):
                    hi, lo = xsp[:, img, j, 0, g], xsp[:, img, j, 1, g]
                    wh, wl = wqh[:, g, h * P:(h + 1) * P], wql[:, g, h * P:(h + 1) * P]
                    T.matmul(ps[:, 2 + h, :], wh, hi, start=(g == 0), stop=False)
                    T.matmul(ps[:, 2 + h, :], wh, lo, start=False, stop=False)
                    last = T.matmul(ps[:, 2 + h, :], wl, hi, start=False, stop=(g == H - 1))
                last.then_inc(s_q, 1)

            def outputs(b, j, g, slot):
                for n in range(2):
                    acc = ps[:, 4 + 2 * g + n, 0:C1]
                    at = slice((2 * g + n) * P, (2 * g + n + 1) * P)
                    for h in range(H):
                        mh, ml = mt[:, h, 0, 0:C1], mt[:, h, 1, 0:C1]
                        T.matmul(acc, qhi[:, slot, h, at], mh, start=(h == 0), stop=False)
                        T.matmul(acc, qhi[:, slot, h, at], ml, start=False, stop=False)
                        last = T.matmul(acc, qlo[:, slot, h, at], mh, start=False, stop=(h == H - 1))
                last.then_inc(s_y, 1)

            def turn_back(b, j, slot):
                pe.wait_ge(s_yt, 1 + 2 * (b * NCH + j + 1))
                for h in range(H):
                    for n in range(4):
                        last = T.transpose(ps[:, h, n * P:(n + 1) * P],
                                           yt[:, slot, n // 2, n % 2, h * P:(h + 1) * P], ident[:, :])
                last.then_inc(s_fin, 1)

            def image(b, last_image=False):
                img = b & 1
                keys(b, 0, 1)
                for n in range(2):
                    sums(b, 0, n, first=(n == 0))
                    keys(b, 1, n)
                with pe.Fori(1, NCH - 1) as j:
                    for n in range(2):
                        sums(b, j, n)
                        keys(b, j + 1, n)
                sums(b, NCH - 1, 0)
                sums(b, NCH - 1, 1, final=True)

                queries(img, 0, 0)
                queries(img, 0, 1)
                pe.wait_ge(s_kx0, b + 1)
                pe.wait_ge(s_kx1, b + 1)
                turn(4, kx[:, :, :, 0:P]).then_inc(s_kxT, 1)
                pe.wait_ge(s_qlo, H * (b * NCH) + 1)
                queries(img, 1, 0)
                pe.wait_ge(s_kxt, b + 1)
                for h in range(H):
                    for g in range(H):
                        last = T.matmul(ps_m[:, h, :], kxt[:, g, h * P:(h + 1) * P], pvt[:, g, :],
                                        start=(g == 0), stop=(g == H - 1))
                last.then_inc(s_m, 1)
                pe.wait_ge(s_qlo, H * (b * NCH) + 2)
                queries(img, 1, 1)
                pe.wait_ge(s_mlo, b + 1)
                pe.wait_ge(s_qlo, H * (b * NCH + 1))
                outputs(b, 0, 0, 0)
                outputs(b, 0, 1, 0)

                def chunk(j, odd, last=False):
                    if not last:
                        pe.wait_ge(s_qlo, H * (b * NCH + j) + 1)
                        queries(img, j + 1, 0)
                    pe.wait_ge(s_qlo, H * (b * NCH + j + 1))
                    pe.wait_ge(s_yt, 2 * (b * NCH + j))
                    outputs(b, j, 0, odd)
                    pe.wait_ge(s_out, 2 + H * (b * NCH + j - 1))
                    turn_back(b, j - 1, 1 - odd)
                    if not last:
                        queries(img, j + 1, 1)
                    outputs(b, j, 1, odd)

                with pe.Fori(0, NCH // 2 - 1) as i:
                    chunk(2 * i + 1, 1)
                    chunk(2 * i + 2, 0)
                chunk(NCH - 1, 1, last=True)
                if not last_image:
                    pe.wait_ge(s_yt, 2 * NCH * (b + 1))
                    keys(b + 1, 0, 0)
                pe.wait_ge(s_out, 2 + H * (b * NCH + NCH - 1))
                turn_back(b, NCH - 1, 1)

            keys(0, 0, 0)
            with pe.Fori(0, B - 1) as b:
                image(b)
            image(B - 1, last_image=True)


def newton(V, step, r, v, t1, t2, res):
    step(V.tensor_tensor(t1, r, r, ALU.mult))
    step(V.tensor_tensor(t2, t1, v, ALU.mult))
    step(V.tensor_scalar(t1, t2, -0.5, 1.5, ALU.mult, ALU.add))
    step(V.tensor_tensor(res, r, t1, ALU.mult))


_INS = ["x", "L0_conv_w_qkv", "L0_conv_w_proj", "L0_conv_bn_gamma", "L0_conv_bn_beta", "L0_conv_bn_mean",
        "L0_conv_bn_var"]


def kernel(**inputs):
    import concourse.bacc as bacc
    from concourse.bass_utils import run_bass_kernel_spmd

    nc = bacc.Bacc("TRN2", target_bir_lowering=False, num_devices=1)
    arrays, args = {}, []
    for name in _INS:
        a = np.ascontiguousarray(inputs[name])
        arrays[f"in_{name}"] = a
        args.append(nc.dram_tensor(f"in_{name}", a.shape, mybir.dt.from_np(a.dtype), kind="ExternalInput").ap())
    out = nc.dram_tensor("out_0", arrays["in_x"].shape, F32, kind="ExternalOutput").ap()
    attention_program(nc, *args, out)
    r = run_bass_kernel_spmd(nc, [arrays], core_ids=[0])
    return r.results[0]["out_0"]
```

```python
import concourse.bass as bass
import numpy as np
from concourse import mybir
from contextlib import ExitStack

F32 = mybir.dt.float32
F16 = mybir.dt.float16
ALU = mybir.AluOpType
ACT = mybir.ActivationFunctionType
AX = mybir.AxisListType.X

P = 128
GROUPS = 32
GN_EPS = 1e-5
BN_EPS = 1e-5
ATT_EPS = 1e-5
TINY = 1e-30


def attention_program(nc, x, w_qkv, w_proj, gamma, beta, bn_mean, bn_var, out):
    B, C, HH, WW = x.shape
    N = HH * WW
    H = C // P
    PER = C // GROUPS
    CH = 512
    NCH = N // CH
    PAIR = 2 * P
    NP = N // PAIR
    KAPPA = 1.0 / (4 * N)
    C1 = C + 1
    CB = CH // P
    P1 = P + 1
    TP = P + 16

    xd = x.rearrange("b (h p) y z -> b p h (y z)", p=P)
    od = out.rearrange("b (h p) y z -> b p h (y z)", p=P)
    wqkv_d = w_qkv.rearrange("(h p j) i -> p h (j i)", p=P, j=3)
    wproj_d = w_proj.rearrange("(h p) i -> p h i", p=P)

    ctx = ExitStack()
    with ctx:
        def sb(name, shape, dt=F32):
            return ctx.enter_context(nc.sbuf_tensor(name, shape, dt))

        def sem(name):
            return ctx.enter_context(nc.semaphore(name))

        xs = sb("xs", [P, 2, H, N])
        xsp = sb("xsp", [P, 2, NCH, 2, H, CH], F16)
        xn = sb("xn", [P, 2, H, CH])
        khi = sb("khi", [P, 2, 2, C], F16)
        klo = sb("klo", [P, 2, 2, C], F16)
        xt = sb("xt", [P, NCH, 2, H, CB, TP], F16)
        work = sb("work", [P, 16 * C])
        yt = work[:, 0:8 * C].rearrange("p (s g n c) -> p s g n c", s=2, g=2, n=2)
        q_split = work[:, 8 * C:16 * C].bitcast(F16).rearrange("p (l s h c) -> p l s h c", l=2, s=2, h=H)
        qhi, qlo = q_split[:, 0], q_split[:, 1]
        w3 = work[:, 0:6 * C].rearrange("p (h c) -> p h c", h=H)
        wn = work[:, 6 * C:10 * C].rearrange("p (j h c) -> p j h c", j=2, h=H)
        wp = work[:, 10 * C:12 * C].rearrange("p (h c) -> p h c", h=H)
        wpt = work[:, 12 * C:14 * C].rearrange("p (h c) -> p h c", h=H)
        pv = work[:, 14 * C:16 * C].rearrange("p (h c) -> p h c", h=H)
        rden = sb("rden", [P, 2, 2])
        den = sb("den", [P, 2, 2])
        kx = sb("kx", [P, H, H, P1])
        kxt = sb("kxt", [P, H, C])
        mt = sb("mt", [P, H, 2, C + 2], F16)
        wqh = sb("wqh", [P, H, C], F16)
        wql = sb("wql", [P, H, C], F16)
        wkh = sb("wkh", [P, H, C], F16)
        wkl = sb("wkl", [P, H, C], F16)
        pvt = sb("pvt", [P, H, C])
        ident = sb("ident", [P, P])
        bn = sb("bn", [P, 4, H])
        rmax = sb("rmax", [P, 2, H])
        rinv = sb("rinv", [P, 2, H])
        pmax = sb("pmax", [P, H])
        pinv = sb("pinv", [P, H])
        rr = sb("rr", [P, H])
        rrm = sb("rrm", [P, 1])
        rall = sb("rall", [P, 1])
        rallc = sb("rallc", [P, 1])
        rallinv = sb("rallinv", [P, 1])
        rho = sb("rho", [P, H])
        deps = sb("deps", [P, 1])
        bs = sb("bs", [P, 8, H])
        oscale = sb("oscale", [P, H])
        obias = sb("obias", [P, H])
        bst = sb("bst", [P, H, NCH, 6])
        cst = sb("cst", [P, 32])
        cstT = sb("cstT", [P, 32])
        gsum = sb("gsum", [P, 32 // PER])
        gexp = sb("gexp", [P, 2, 32])
        gdev = sb("gdev", [P, 32])
        gsq = sb("gsq", [P, 32])
        gsum2 = sb("gsum2", [P, 32 // PER])
        gback = sb("gback", [P, 2, 32])
        gvar = sb("gvar", [P, H])
        gstd = sb("gstd", [P, H])
        nr = sb("nr", [P, 4, H])
        gmean = sb("gmean", [P, H])
        grstd = sb("grstd", [P, H])

        ps = ctx.enter_context(nc.psum_tensor("ps", [P, 8, 512], F32))

        def ps_k(slot):
            return ps[:, 4 + 2 * slot, :].rearrange("p (n c) -> p n c", n=2)

        def ps_sum(h):
            return ps[:, h, 0:H * P1].rearrange("p (g c) -> p g c", g=H)

        ps_kxt = ps[:, 4, :].rearrange("p (g c) -> p g c", g=H)
        ps_m = ps[:, 6:6 + H, 0:C]

        s_w3 = sem("s_w3")
        s_wp = sem("s_wp")
        s_w = sem("s_w")
        s_id = sem("s_id")
        s_wmax = sem("s_wmax")
        s_wabs = sem("s_wabs")
        s_wt = sem("s_wt")
        s_wthi = sem("s_wthi")
        s_wtlo = sem("s_wtlo")
        s_pv = sem("s_pv")
        s_pvn = sem("s_pvn")
        s_rrm = sem("s_rrm")
        s_rall = sem("s_rall")
        s_bnv = sem("s_bnv")
        s_bnsqrt = sem("s_bnsqrt")
        s_consts = sem("s_consts")
        s_set = sem("s_set")
        s_first = [sem(f"s_first{j}") for j in range(NCH)]
        s_load = sem("s_load")
        s_store = sem("s_store")
        s_bst = sem("s_bst")
        s_stat = sem("s_stat")
        s_gvar = sem("s_gvar")
        s_gstd = sem("s_gstd")
        s_xn = sem("s_xn")
        s_xn0 = sem("s_xn0")
        s_xhi0 = sem("s_xhi0")
        s_xhi = sem("s_xhi")
        s_xlo = sem("s_xlo")
        s_stood = sem("s_stood")
        s_stood_v = sem("s_stood_v")
        s_xt = sem("s_xt")
        s_kx = sem("s_kx")
        s_khi = sem("s_khi")
        s_klo = sem("s_klo")
        s_sum = sem("s_sum")
        s_kx0 = sem("s_kx0")
        s_kx1 = sem("s_kx1")
        s_kxT = sem("s_kxT")
        s_kxt = sem("s_kxt")
        s_m = sem("s_m")
        s_mhi = sem("s_mhi")
        s_mlo = sem("s_mlo")
        s_mk = sem("s_mk")
        s_q = sem("s_q")
        s_qhi = sem("s_qhi")
        s_qlo = sem("s_qlo")
        s_y = sem("s_y")
        s_dsum = sem("s_dsum")
        s_rden = sem("s_rden")
        s_yt = sem("s_yt")
        s_fin = sem("s_fin")
        s_out = sem("s_out")
        s_xb = sem("s_xb")

        SMALL_LOADS = 4
        EARLY = 3

        block = ctx.enter_context(nc.Block())

        @block.sync
        def _(sp):
            def load(b, slot, c0, landed=s_load):
                sp.dma_start(xs[:, slot, :, bass.ds(c0, CH)],
                             xd[b, :, :, bass.ds(c0, CH)]).then_inc(landed, 16)

            def transpose(b, j, slot):
                sp.wait_ge(s_xlo, NCH * b + j + 1)
                sp.sem_inc(s_stood, 1)
                if not isinstance(b, int) or b:
                    sp.wait_ge(s_sum, NP * b)
                    sp.sem_inc(s_stood, 1)
                if not isinstance(b, int) or b or j:
                    sp.wait_ge(s_xt, 16 * (NCH * b + j))
                    sp.sem_inc(s_stood, 1)
                sp.dma_start_transpose(xt[:, j].rearrange("p s h n c -> p (s h n) c")[:, :, 0:P],
                                       xsp[:, slot, j].rearrange("p s h c -> p (s h c)")
                                       ).then_inc(s_xt, 16)

            def store(b, j, slot):
                sp.wait_ge(s_out, 2 + H * (b * NCH + j + 1))
                sp.dma_start(od[b, :, :, bass.ds(j * CH, CH)],
                             xs[:, slot, :, bass.ds(j * CH, CH)]).then_inc(s_store, 16)

            sp.dma_start(w3[:, :, :], wqkv_d).then_inc(s_w3, 16)
            for j in range(NCH):
                load(0, 0, j * CH, s_first[j])
            for j in range(NCH):
                transpose(0, j, 0)
                if j:
                    sp.wait_ge(s_load, 16 * j)
                load(1, 1, j * CH)

            with sp.Fori(0, B - 2) as b:
                slot = b & 1
                with sp.Fori(0, NCH) as j:
                    transpose(b + 1, j, 1 - slot)
                    store(b, j, slot)
                    sp.wait_ge(s_load, 16 * (NCH * (b + 1) + j))
                    sp.sem_inc(s_stood, 1)
                    sp.wait_ge(s_store, 16 * (b * NCH + j + 1))
                    load(b + 2, slot, j * CH)
            with sp.Fori(0, NCH) as j:
                transpose(B - 1, j, (B - 1) & 1)
                store(B - 2, j, (B - 2) & 1)
            with sp.Fori(0, NCH) as j:
                store(B - 1, j, (B - 1) & 1)
            sp.wait_ge(s_store, 16 * NCH * B)

        @block.gpsimd
        def _(pool):
            nc.gpsimd.memset(ident[:, :], 0.0).then_inc(s_id, 1)
            pool.wait_ge(s_id, 1)
            nc.gpsimd.affine_select(out=ident[:, :], in_=ident[:, :], compare_op=ALU.not_equal, fill=1.0,
                                    base=0, pattern=[[-1, P]], channel_multiplier=1).then_inc(s_id, 1)
            pool.wait_ge(s_rrm, 1)
            nc.gpsimd.partition_all_reduce(rall[:, :], rrm[:, :], P, bass.bass_isa.ReduceOp.max
                                           ).then_inc(s_rall, 1)

            def split_lo(b, j, slot, buf):
                pool.wait_ge(s_xhi, b * NCH + j + 1)
                nc.gpsimd.tensor_tensor(xsp[:, slot, j, 1], xn[:, buf], xsp[:, slot, j, 0], ALU.subtract
                                        ).then_inc(s_xlo, 1)

            pool.wait_ge(s_xlo, 1)
            for j in range(1, NCH):
                split_lo(0, j, 0, j % 2)
            with pool.Fori(1, B) as b:
                with pool.Fori(0, NCH // 2) as i:
                    split_lo(b, 2 * i, b & 1, 0)
                    split_lo(b, 2 * i + 1, b & 1, 1)

        @block.scalar
        def _(act):
            act.dma_start(wp[:, :, :], wproj_d).then_inc(s_wp, 16)
            for n, v in enumerate((gamma, beta, bn_mean, bn_var)):
                act.dma_start(bn[:, n, :], v.rearrange("(h p) -> p h", p=P),
                              allow_slow_non_contiguous=True).then_inc(s_w, 16)
            for n, dst in enumerate((wkh, wqh, wpt)):
                act.wait_ge(s_wt, n + 1)
                nc.scalar.copy(dst[:, :, :], ps[:, 2 + n, :].rearrange("p (g c) -> p g c", g=H)
                               ).then_inc(s_wthi, 1)
            act.sem_inc(s_yt, 1)
            act.wait_ge(s_bnv, 1)
            nc.scalar.activation(bs[:, 1, :], bs[:, 0, :], ACT.Sqrt).then_inc(s_bnsqrt, 1)

            def group_std(b):
                act.wait_ge(s_gvar, b + 1)
                nc.scalar.activation(gstd[:, :], gvar[:, :], ACT.Sqrt).then_inc(s_gstd, 1)

            def split_hi(b, j, slot, buf):
                act.wait_ge(s_xn, b * NCH + j + 1)
                nc.scalar.copy(xsp[:, slot, j, 0], xn[:, buf]).then_inc(s_xhi, 1)

            def k_hi(b, t, slot):
                act.wait_ge(s_kx, b * NP + t + 1)
                if not isinstance(t, int) or t >= 2:
                    act.wait_ge(s_sum, b * NP + t - 1)
                nc.scalar.activation(khi[:, slot], ps_k(slot), ACT.Relu).then_inc(s_khi, 1)

            def add_bias(b, j, slot):
                act.wait_ge(s_xlo, b * NCH + j + 1)
                for h in range(H):
                    last = nc.scalar.activation(xs[:, slot, h, bass.ds(j * CH, CH)],
                                                xs[:, slot, h, bass.ds(j * CH, CH)],
                                                ACT.Identity, bias=obias[:, h:h + 1], scale=1.0)
                last.then_inc(s_xb, 1)

            def q_hi(b, j, h, slot):
                act.wait_ge(s_q, H * (b * NCH + j) + h + 1)
                nc.scalar.activation(qhi[:, slot, h, :], ps[:, 2 + h, :], ACT.Relu).then_inc(s_qhi, 1)

            def divide(b, j, g, slot):
                act.wait_ge(s_rden, 2 * (b * NCH + j) + g + 1)
                for n in range(2):
                    last = nc.scalar.activation(yt[:, slot, g, n, :], ps[:, 4 + 2 * g + n, 0:C], ACT.Copy,
                                                scale=rden[:, g, n:n + 1])
                last.then_inc(s_yt, 1)

            def image(b, prepare, first=False):
                slot, other = b & 1, 1 - (b & 1)
                if first:
                    for t in range(1, NCH):
                        k_hi(b, t, t % 2)
                        j = EARLY + t - 2
                        if EARLY <= j < NCH:
                            split_hi(0, j, 0, j % 2)
                    act.wait_ge(s_consts, 1)
                    for j in range(2):
                        add_bias(b, j, slot)
                    with act.Fori(NCH // 2, NCH - 1) as i:
                        for n in range(2):
                            k_hi(b, 2 * i + n, n)
                            add_bias(b, 2 * i + n - NCH + 2, slot)
                else:
                    k_hi(b, 1, 1)
                    k_hi(b, 2, 0)
                    split_hi(b, NCH - 1, slot, 1)
                    add_bias(b, 0, slot)
                    k_hi(b, 3, 1)
                    add_bias(b, 1, slot)
                    with act.Fori(2, NCH - 1) as i:
                        k_hi(b, 2 * i, 0)
                        k_hi(b, 2 * i + 1, 1)
                        add_bias(b, i, slot)
                if prepare:
                    group_std(b + 1)
                k_hi(b, NP - 2, 0)
                k_hi(b, NP - 1, 1)
                q_hi(b, 0, 0, 0)
                act.wait_ge(s_sum, NP * (b + 1))
                nc.scalar.activation(kx[:, 0], ps_sum(0), ACT.Copy,
                                     scale=rho[:, 0:1]).then_inc(s_kx0, 1)
                q_hi(b, 0, 1, 0)
                if not first:
                    add_bias(b, NCH - 1, slot)
                q_hi(b, 1, 0, 1)
                for h in range(H):
                    act.wait_ge(s_m, H * b + h + 1)
                    nc.scalar.copy(mt[:, h, 0, 0:C], ps_m[:, h]).then_inc(s_mhi, 1)
                q_hi(b, 1, 1, 1)
                divide(b, 0, 0, 0)
                divide(b, 0, 1, 0)

                def chunk(j, odd):
                    q_hi(b, j + 1, 0, 1 - odd)
                    if prepare:
                        split_hi(b + 1, j - 1, other, 1 - odd)
                    divide(b, j, 0, odd)
                    q_hi(b, j + 1, 1, 1 - odd)
                    divide(b, j, 1, odd)

                with act.Fori(0, NCH // 2 - 1) as i:
                    chunk(2 * i + 1, 1)
                    chunk(2 * i + 2, 0)
                divide(b, NCH - 1, 0, 1)
                divide(b, NCH - 1, 1, 1)
                if prepare:
                    split_hi(b + 1, NCH - 2, other, 0)
                    k_hi(b + 1, 0, 0)

            group_std(0)
            for h in range(H):
                act.wait_ge(s_xn0, h + 1)
                nc.scalar.copy(xsp[:, 0, 0, 0, h, :], xn[:, 0, h, :]).then_inc(s_xhi0, 1)
            act.sem_inc(s_xhi, 1)
            split_hi(0, 1, 0, 1)
            k_hi(0, 0, 0)
            split_hi(0, 2, 0, 0)
            act.wait_ge(s_wt, 4)
            nc.scalar.copy(pvt[:, :, :], ps[:, 7, :].rearrange("p (g c) -> p g c", g=H)
                           ).then_inc(s_wthi, 1)
            image(0, True, first=True)
            with act.Fori(1, B - 1) as b:
                image(b, True)
            image(B - 1, False)

        @block.vector
        def _(dve):
            set_up = [0]

            def step(ins):
                set_up[0] += 1
                ins.then_inc(s_set, 1)
                dve.wait_ge(s_set, set_up[0])

            V = nc.vector
            for n in range(2):
                V.memset(xt[:, n * NCH // 2:(n + 1) * NCH // 2].rearrange("p j s h n c -> p (j s h n) c")[:, :, P:P1],
                         1.0).then_inc(s_out, 1)

            def weights_scale():
                def largest():
                    dve.wait_ge(s_w3, 16)
                    for h in range(H):
                        V.tensor_reduce(rmax[:, :, h], w3[:, h, 0:2 * C].rearrange("p (j i) -> p j i", j=2),
                                        AX, ALU.max, apply_absolute_value=True).then_inc(s_wmax, 1)

                def floored():
                    dve.wait_ge(s_wmax, H)
                    V.tensor_scalar_max(rmax[:, :, :], rmax[:, :, :], TINY).then_inc(s_wmax, 1)

                def inverted():
                    dve.wait_ge(s_wmax, H + 1)
                    V.reciprocal(rinv[:, :, :], rmax[:, :, :]).then_inc(s_wmax, 1)
                    V.tensor_tensor(rr[:, :], rmax[:, 0, :], rmax[:, 1, :], ALU.mult).then_inc(s_wmax, 1)

                def scaled():
                    dve.wait_ge(s_wmax, H + 3)
                    for j in (1, 0):
                        for h in range(H):
                            V.tensor_scalar(wn[:, j, h, :], w3[:, h, j * C:(j + 1) * C], rinv[:, j, h:h + 1],
                                            None, ALU.mult).then_inc(s_wabs, 1)
                    V.tensor_reduce(rrm[:, :], rr[:, :], AX, ALU.max).then_inc(s_rrm, 1)

                return largest, floored, inverted, scaled

            def batch_variance():
                dve.wait_ge(s_w, 16 * SMALL_LOADS)
                V.tensor_scalar(bs[:, 0, :], bn[:, 3, :], BN_EPS, None, ALU.add).then_inc(s_bnv, 1)

            def split_weights(n, hi, lo):
                dve.wait_ge(s_wthi, n + 1)
                V.tensor_tensor(lo[:, :, :], ps[:, 2 + n, :].rearrange("p (g c) -> p g c", g=H),
                                hi[:, :, :], ALU.subtract).then_inc(s_wtlo, 1)

            def projection():
                dve.wait_ge(s_pv, 1)
                ps_pv = ps[:, 5, :].rearrange("p (h c) -> p h c", h=H)
                step(V.tensor_reduce(pmax[:, :], ps_pv, AX, ALU.max, apply_absolute_value=True))
                step(V.tensor_scalar_max(pmax[:, :], pmax[:, :], TINY))
                step(V.reciprocal(pinv[:, :], pmax[:, :]))
                for h in range(H):
                    V.tensor_scalar(pv[:, h, :], ps_pv[:, h, :], pinv[:, h:h + 1], None,
                                    ALU.mult).then_inc(s_pvn, 1)

            def vectors():
                dve.wait_ge(s_bnsqrt, 1)
                step(V.reciprocal(bs[:, 2, :], bs[:, 1, :]))
                newton(V, step, bs[:, 2, :], bs[:, 0, :], bs[:, 3, :], bs[:, 4, :], bs[:, 5, :])
                step(V.tensor_tensor(bs[:, 6, :], bs[:, 5, :], bn[:, 0, :], ALU.mult))
                step(V.tensor_tensor(bs[:, 7, :], bs[:, 6, :], bn[:, 2, :], ALU.mult))
                step(V.tensor_tensor(obias[:, :], bn[:, 1, :], bs[:, 7, :], ALU.subtract))
                step(V.tensor_tensor(oscale[:, :], pmax[:, :], bs[:, 6, :], ALU.mult))
                dve.wait_ge(s_rall, 1)
                step(V.tensor_scalar_max(rallc[:, :], rall[:, :], TINY))
                step(V.reciprocal(rallinv[:, :], rallc[:, :]))
                step(V.tensor_scalar(rho[:, :], rr[:, :], rallinv[:, 0:1], KAPPA, ALU.mult, ALU.mult))
                V.tensor_scalar(deps[:, :], rallinv[:, :], ATT_EPS * KAPPA, None, ALU.mult).then_inc(s_consts, 1)
                dve.wait_ge(s_consts, 1)

            def channel_stats(slot, j, h):
                V.bn_stats(bst[:, h, j, :], xs[:, slot, h, bass.ds(j * CH, CH)]).then_inc(s_bst, 1)

            STAT_STEPS = 17

            def group_stats(b):
                done = [0]

                def step(ins, read_next=True):
                    done[0] += 1
                    ins.then_inc(s_stat, 1)
                    if read_next:
                        dve.wait_ge(s_stat, STAT_STEPS * b + done[0])

                def first():
                    dve.wait_ge(s_bst, H * NCH * (b + 1))
                    step(V.memset(cst[:, 2 * H:], 0.0), False)
                    for h in range(H):
                        step(V.bn_aggr(cst[:, 2 * h:2 * h + 2], bst[:, h, :, :].rearrange("p n s -> p (n s)")),
                             h == H - 1)
                    step(V.transpose(cstT[:, :], cst[:, :]))
                    groups = "p (g e) -> p g e"
                    step(V.reduce_sum(gsum[:, :], cstT[:, :].rearrange(groups, e=PER), AX))
                    step(V.tensor_scalar(gexp[:, 0, :].rearrange(groups, e=PER),
                                         gsum[:, :].unsqueeze(2).to_broadcast([P, 32 // PER, PER]),
                                         1.0 / PER, None, ALU.mult))

                def second():
                    groups = "p (g e) -> p g e"
                    step(V.tensor_tensor(gdev[:, :], cstT[:, :], gexp[:, 0, :], ALU.subtract))
                    step(V.tensor_tensor(gsq[:, :], gdev[:, :], gdev[:, :], ALU.mult))
                    step(V.reduce_sum(gsum2[:, :], gsq[:, :].rearrange(groups, e=PER), AX))
                    step(V.tensor_scalar(gexp[:, 1, :].rearrange(groups, e=PER),
                                         gsum2[:, :].unsqueeze(2).to_broadcast([P, 32 // PER, PER]),
                                         1.0 / PER, None, ALU.mult))
                    step(V.transpose(gback[:, :, :].rearrange("p s c -> p (s c)"),
                                     gexp[:, :, :].rearrange("p s c -> p (s c)")))
                    step(V.tensor_copy(gmean[:, :], gback[:, 0, 0:2 * H:2]))
                    V.scalar_tensor_tensor(gvar[:, :], gback[:, 0, 1:2 * H:2], GN_EPS, gback[:, 1, 0:2 * H:2],
                                           ALU.add, ALU.add).then_inc(s_gvar, 1)

                def third():
                    dve.wait_ge(s_gstd, b + 1)
                    step(V.reciprocal(nr[:, 0, :], gstd[:, :]))
                    newton(V, step, nr[:, 0, :], gvar[:, :], nr[:, 1, :], nr[:, 2, :], grstd[:, :])
                    assert done[0] == STAT_STEPS

                return first, second, third

            def normalise(b, j, slot, buf):
                if not isinstance(b, int) or b > 0 or not isinstance(j, int) or j >= 2:
                    dve.wait_ge(s_xlo, b * NCH + j - 1)
                    dve.sem_inc(s_stood_v, 1)
                for h in range(H):
                    last = V.tensor_scalar(xn[:, buf, h, :], xs[:, slot, h, bass.ds(j * CH, CH)],
                                           gmean[:, h:h + 1], grstd[:, h:h + 1], ALU.subtract, ALU.mult)
                last.then_inc(s_xn, 1)

            def k_lo(b, t, slot):
                dve.wait_ge(s_khi, b * NP + t + 1)
                V.scalar_tensor_tensor(klo[:, slot], ps_k(slot), 0.0, khi[:, slot],
                                       ALU.max, ALU.subtract).then_inc(s_klo, 1)

            def q_lo(b, j, h, slot):
                dve.wait_ge(s_qhi, H * (b * NCH + j) + h + 1)
                V.scalar_tensor_tensor(qlo[:, slot, h, :], ps[:, 2 + h, :], 0.0, qhi[:, slot, h, :],
                                       ALU.max, ALU.subtract).then_inc(s_qlo, 1)

            def denominators(b, j, g):
                pair = 2 * (b * NCH + j) + g
                dve.wait_ge(s_y, pair + 1)
                V.tensor_scalar(den[:, g, :], ps[:, 4 + 2 * g:6 + 2 * g, C], deps[:, 0:1], None,
                                ALU.add).then_inc(s_dsum, 1)
                dve.wait_ge(s_dsum, pair + 1)
                V.reciprocal(rden[:, g, :], den[:, g, :]).then_inc(s_rden, 1)

            def finish(b, j, slot):
                dve.wait_ge(s_fin, b * NCH + j + 1)
                for h in range(H):
                    V.scalar_tensor_tensor(xs[:, slot, h, bass.ds(j * CH, CH)], ps[:, h, :], oscale[:, h:h + 1],
                                           xs[:, slot, h, bass.ds(j * CH, CH)], ALU.mult, ALU.add
                                           ).then_inc(s_out, 1)

            def image(b, prepare, first=False):
                slot, other = b & 1, 1 - (b & 1)
                for t in range(1, 4):
                    k_lo(b, t, t % 2)
                    if first:
                        normalise(0, EARLY + t - 1, 0, (EARLY + t - 1) % 2)
                    elif t == 1:
                        normalise(b, NCH - 1, slot, 1)

                def pair(i, n):
                    k_lo(b, 2 * i + 4 + n, n)
                    if prepare:
                        dve.wait_ge(s_load, 16 * (NCH * b + 2 * i + n + 1))
                        dve.sem_inc(s_stood_v, 1)
                        for h in range(H):
                            channel_stats(other, 2 * i + n, h)

                if first:
                    for n in range(2):
                        pair(0, n)
                        j = EARLY + 3 + n
                        normalise(0, j, 0, j % 2)
                with dve.Fori(1 if first else 0, NCH // 2) as i:
                    for n in range(2):
                        pair(i, n)
                stages = group_stats(b + 1) if prepare else ()
                for n in range(4):
                    k_lo(b, NP - 4 + n, n % 2)
                    if prepare and n < 3:
                        stages[n]()
                q_lo(b, 0, 0, 0)
                dve.wait_ge(s_sum, NP * (b + 1))
                V.tensor_scalar(kx[:, 1], ps_sum(1), rho[:, 1:2], None, ALU.mult).then_inc(s_kx1, 1)
                dve.wait_ge(s_kx0, b + 1)
                dve.wait_ge(s_kx1, b + 1)
                V.tensor_copy(mt[:, :, 0, C:C1], kx[:, :, 0, P:P1]).then_inc(s_mk, 1)
                dve.wait_ge(s_mk, b + 1)
                V.tensor_tensor(mt[:, :, 1, C:C1], kx[:, :, 0, P:P1], mt[:, :, 0, C:C1], ALU.subtract)
                dve.wait_ge(s_kxT, b + 1)
                V.tensor_copy(kxt[:, :, :], ps_kxt).then_inc(s_kxt, 1)
                q_lo(b, 0, 1, 0)
                q_lo(b, 1, 0, 1)
                for h in range(H):
                    dve.wait_ge(s_mhi, H * b + h + 1)
                    V.tensor_tensor(mt[:, h, 1, 0:C], ps_m[:, h], mt[:, h, 0, 0:C], ALU.subtract
                                    ).then_inc(s_mlo, 1)
                q_lo(b, 1, 1, 1)
                denominators(b, 0, 0)
                denominators(b, 0, 1)
                dve.wait_ge(s_xb, NCH * (b + 1))
                if prepare:
                    normalise(b + 1, 0, other, 0)

                def chunk(j, odd):
                    q_lo(b, j + 1, 0, 1 - odd)
                    denominators(b, j, 0)
                    if prepare:
                        normalise(b + 1, j, other, odd)
                    q_lo(b, j + 1, 1, 1 - odd)
                    denominators(b, j, 1)
                    finish(b, j - 1, slot)

                with dve.Fori(0, NCH // 2 - 1) as i:
                    chunk(2 * i + 1, 1)
                    chunk(2 * i + 2, 0)
                denominators(b, NCH - 1, 0)
                denominators(b, NCH - 1, 1)
                finish(b, NCH - 2, slot)
                if prepare:
                    k_lo(b + 1, 0, 0)
                finish(b, NCH - 1, slot)

            between = list(weights_scale())
            between.pop(0)()
            for j in range(NCH):
                dve.wait_ge(s_first[j], 16)
                for h in range(H):
                    channel_stats(0, j, h)
                    if between:
                        between.pop(0)()
                if j == NCH // 2:
                    batch_variance()
                if j == NCH // 2 + 1:
                    split_weights(0, wkh, wkl)
            for stage in group_stats(0):
                stage()
            for h in range(H):
                V.tensor_scalar(xn[:, 0, h, :], xs[:, 0, h, 0:CH], gmean[:, h:h + 1], grstd[:, h:h + 1],
                                ALU.subtract, ALU.mult).then_inc(s_xn0, 1)
            dve.sem_inc(s_xn, 1)
            for h in range(H):
                dve.wait_ge(s_xhi0, h + 1)
                last = V.tensor_tensor(xsp[:, 0, 0, 1, h, :], xn[:, 0, h, :], xsp[:, 0, 0, 0, h, :], ALU.subtract)
            last.then_inc(s_xlo, 1)
            normalise(0, 1, 0, 1)
            projection()
            split_weights(1, wqh, wql)
            k_lo(0, 0, 0)
            normalise(0, 2, 0, 0)
            vectors()
            image(0, True, first=True)
            with dve.Fori(1, B - 1) as b:
                image(b, True)
            image(B - 1, False)

        @block.tensor
        def _(pe):
            T = nc.tensor

            def halves(src):
                return src.rearrange("p h (g c) -> p h g c", g=H)

            def turn(bank, src):
                dst = ps[:, bank, :].rearrange("p (g c) -> p g c", g=H)
                for g in range(H):
                    for h in range(H):
                        last = T.transpose(dst[:, g, h * P:(h + 1) * P], src[:, h, g, :], ident[:, :])
                return last

            pe.wait_ge(s_id, 2)
            pe.wait_ge(s_wabs, 2)
            turn(2, halves(wn[:, 1])).then_inc(s_wt, 1)
            pe.wait_ge(s_wabs, 4)
            turn(3, halves(wn[:, 0])).then_inc(s_wt, 1)
            pe.wait_ge(s_wp, 16)
            turn(4, halves(wp)).then_inc(s_wt, 1)
            pe.wait_ge(s_wthi, 3)
            for h in range(H):
                for g in range(H):
                    last = T.matmul(ps[:, 5, h * C:(h + 1) * C], wpt[:, g, h * P:(h + 1) * P],
                                    w3[:, g, 2 * C:3 * C], start=(g == 0), stop=(g == H - 1))
            last.then_inc(s_pv, 1)
            pe.wait_ge(s_wtlo, 1)

            def keys(b, j, slot):
                if slot == 0:
                    pe.wait_ge(s_xlo, b * NCH + j + 1)
                x_hi, x_lo = xsp[:, b & 1, j, 0], xsp[:, b & 1, j, 1]
                for n in range(2):
                    at = slice((2 * slot + n) * P, (2 * slot + n + 1) * P)
                    k_out = ps_k(slot)[:, n, :]
                    for g in range(H):
                        T.matmul(k_out, x_hi[:, g, at], wkh[:, g, :], start=(g == 0), stop=False)
                        T.matmul(k_out, x_hi[:, g, at], wkl[:, g, :], start=False, stop=False)
                        last = T.matmul(k_out, x_lo[:, g, at], wkh[:, g, :], start=False, stop=(g == H - 1))
                last.then_inc(s_kx, 1)

            def sums(b, j, slot, first=False, final=False):
                if first:
                    pe.wait_ge(s_out, 1 + H * NCH * b)
                if slot == 0:
                    pe.wait_ge(s_xt, 16 * (b * NCH + j + 1))
                pe.wait_ge(s_klo, b * NP + 2 * j + slot + 1)
                for n in range(2):
                    ones = xt[:, j, 0, :, 2 * slot + n, 0:P1]
                    lo = xt[:, j, 1, :, 2 * slot + n, 0:P]
                    for h in range(H):
                        if first and n == 0 and h == 1:
                            pe.wait_ge(s_out, 2 + H * NCH * b)
                        kh, kl = khi[:, slot, n, h * P:(h + 1) * P], klo[:, slot, n, h * P:(h + 1) * P]
                        T.matmul(ps_sum(h), kh, ones, start=(first and n == 0), stop=False)
                        T.matmul(ps_sum(h)[:, :, 0:P], kh, lo, start=False, stop=False)
                        last = T.matmul(ps_sum(h), kl, ones, start=False, stop=(final and n == 1))
                last.then_inc(s_sum, 1)

            def queries(img, j, h):
                for g in range(H):
                    hi, lo = xsp[:, img, j, 0, g], xsp[:, img, j, 1, g]
                    wh, wl = wqh[:, g, h * P:(h + 1) * P], wql[:, g, h * P:(h + 1) * P]
                    T.matmul(ps[:, 2 + h, :], wh, hi, start=(g == 0), stop=False)
                    T.matmul(ps[:, 2 + h, :], wh, lo, start=False, stop=False)
                    last = T.matmul(ps[:, 2 + h, :], wl, hi, start=False, stop=(g == H - 1))
                last.then_inc(s_q, 1)

            def outputs(b, j, g, slot):
                for n in range(2):
                    acc = ps[:, 4 + 2 * g + n, 0:C1]
                    at = slice((2 * g + n) * P, (2 * g + n + 1) * P)
                    for h in range(H):
                        mh, ml = mt[:, h, 0, 0:C1], mt[:, h, 1, 0:C1]
                        T.matmul(acc, qhi[:, slot, h, at], mh, start=(h == 0), stop=False)
                        T.matmul(acc, qhi[:, slot, h, at], ml, start=False, stop=False)
                        last = T.matmul(acc, qlo[:, slot, h, at], mh, start=False, stop=(h == H - 1))
                last.then_inc(s_y, 1)

            def turn_back(b, j, slot):
                pe.wait_ge(s_yt, 1 + 2 * (b * NCH + j + 1))
                for h in range(H):
                    pe.wait_ge(s_out, 1 + h + H * (b * NCH + j))
                    for n in range(4):
                        last = T.transpose(ps[:, h, n * P:(n + 1) * P],
                                           yt[:, slot, n // 2, n % 2, h * P:(h + 1) * P], ident[:, :])
                last.then_inc(s_fin, 1)

            def image(b, last_image=False):
                img = b & 1
                keys(b, 0, 1)
                for n in range(2):
                    sums(b, 0, n, first=(n == 0))
                    keys(b, 1, n)
                with pe.Fori(1, NCH - 1) as j:
                    for n in range(2):
                        sums(b, j, n)
                        keys(b, j + 1, n)
                sums(b, NCH - 1, 0)
                queries(img, 0, 0)
                sums(b, NCH - 1, 1, final=True)
                queries(img, 0, 1)
                pe.wait_ge(s_kx0, b + 1)
                pe.wait_ge(s_kx1, b + 1)
                turn(4, kx[:, :, :, 0:P]).then_inc(s_kxT, 1)
                pe.wait_ge(s_qlo, H * (b * NCH) + 1)
                queries(img, 1, 0)
                pe.wait_ge(s_wthi, 4)
                pe.wait_ge(s_kxt, b + 1)
                for h in range(H):
                    for g in range(H):
                        last = T.matmul(ps_m[:, h, :], kxt[:, g, h * P:(h + 1) * P], pvt[:, g, :],
                                        start=(g == 0), stop=(g == H - 1))
                    last.then_inc(s_m, 1)
                pe.wait_ge(s_qlo, H * (b * NCH) + 2)
                queries(img, 1, 1)
                pe.wait_ge(s_mlo, H * (b + 1))
                pe.wait_ge(s_qlo, H * (b * NCH + 1))
                outputs(b, 0, 0, 0)
                outputs(b, 0, 1, 0)

                def chunk(j, odd):
                    pe.wait_ge(s_qlo, H * (b * NCH + j) + 1)
                    queries(img, j + 1, 0)
                    pe.wait_ge(s_qlo, H * (b * NCH + j + 1))
                    pe.wait_ge(s_yt, 2 * (b * NCH + j))
                    outputs(b, j, 0, odd)
                    queries(img, j + 1, 1)
                    pe.wait_ge(s_yt, 1 + 2 * (b * NCH + j))
                    outputs(b, j, 1, odd)
                    turn_back(b, j - 1, 1 - odd)

                with pe.Fori(0, NCH // 2 - 1) as i:
                    chunk(2 * i + 1, 1)
                    chunk(2 * i + 2, 0)
                end = b * NCH + NCH
                pe.wait_ge(s_qlo, H * end)
                pe.wait_ge(s_yt, 2 * (end - 1))
                outputs(b, NCH - 1, 0, 1)
                pe.wait_ge(s_yt, 1 + 2 * (end - 1))
                outputs(b, NCH - 1, 1, 1)
                turn_back(b, NCH - 2, 0)
                if not last_image:
                    pe.wait_ge(s_yt, 2 * NCH * (b + 1))
                    keys(b + 1, 0, 0)
                turn_back(b, NCH - 1, 1)

            keys(0, 0, 0)
            pe.wait_ge(s_pvn, 2)
            turn(7, halves(pv)).then_inc(s_wt, 1)
            pe.wait_ge(s_wtlo, 2)
            with pe.Fori(0, B - 1) as b:
                image(b)
            image(B - 1, last_image=True)


def newton(V, step, r, v, t1, t2, res):
    step(V.tensor_tensor(t1, r, r, ALU.mult))
    step(V.tensor_tensor(t2, t1, v, ALU.mult))
    step(V.tensor_scalar(t1, t2, -0.5, 1.5, ALU.mult, ALU.add))
    step(V.tensor_tensor(res, r, t1, ALU.mult))


_INS = ["x", "L0_conv_w_qkv", "L0_conv_w_proj", "L0_conv_bn_gamma", "L0_conv_bn_beta", "L0_conv_bn_mean",
        "L0_conv_bn_var"]


def kernel(**inputs):
    import concourse.bacc as bacc
    from concourse.bass_utils import run_bass_kernel_spmd

    nc = bacc.Bacc("TRN2", target_bir_lowering=False, num_devices=1)
    arrays, args = {}, []
    for name in _INS:
        a = np.ascontiguousarray(inputs[name])
        arrays[f"in_{name}"] = a
        args.append(nc.dram_tensor(f"in_{name}", a.shape, mybir.dt.from_np(a.dtype), kind="ExternalInput").ap())
    out = nc.dram_tensor("out_0", arrays["in_x"].shape, F32, kind="ExternalOutput").ap()
    attention_program(nc, *args, out)
    r = run_bass_kernel_spmd(nc, [arrays], core_ids=[0])
    return r.results[0]["out_0"]
```
